# Optimizing a Trainium2 kernel written in Bass

```python
import numpy as np
import jax
import jax.numpy as jnp

def _softmax(x, axis=-1):
    return jax.nn.softmax(x, axis=axis)
def _gelu(x):
    return jax.nn.gelu(x, approximate=True)
def _silu(x):
    return jax.nn.silu(x)
def _sigmoid(x):
    return jax.nn.sigmoid(x)
def _layernorm(x, axis=-1, eps=1e-5):
    m = jnp.mean(x, axis=axis, keepdims=True)
    v = jnp.var(x, axis=axis, keepdims=True)
    return (x - m) / jnp.sqrt(v + eps)
def _scatter_add(tgt, idx, src, axis=0):
    return tgt.at[idx].add(src)
def _segment_sum(src, seg, n):
    return jax.ops.segment_sum(src, seg, n)

kernel_name = 'mk_conv_preact_d1_conv_nchw128_15c5c1'

def setup_inputs(seed: int = 0):
    np.random.seed(seed)
    _w = jnp.asarray
    def _rec_inputs():
        import jax
        import jax.numpy as jnp
        _gk = jax.random.key(seed)
        x = -9.26e-05 + 0.9999 * jax.random.normal(jax.random.fold_in(_gk, 1), (128, 128, 48, 48), jnp.float32)
        return x
    x = _rec_inputs()
    def _L0_conv_setup():
        import jax, jax.numpy as jnp
        import numpy as np
        B, H, W = (128, 48, 48)
        CEN_IN, CEN_OUT, DIR_IN, DIR_OUT, CEN_K, DIR_K = (32, 32, 24, 24, 3, 5)
        C_IN = CEN_IN + 4 * DIR_IN

        def _dwconv(x, k):
            C = x.shape[1]
            return jax.lax.conv_general_dilated(x, k[:, None], window_strides=(1, 1), padding='SAME', dimension_numbers=('NCHW', 'OIHW', 'NCHW'), feature_group_count=C)
        key = jax.random.key(seed)
        ks = jax.random.split(key, 8)
        s = 0.1
        return {'x': jax.random.normal(ks[0], (B, C_IN, H, W), dtype=jnp.float32), 'cen_tensor': jax.random.normal(ks[1], (CEN_IN, CEN_K, CEN_K), dtype=jnp.float32) * s, 'dir_tensor': jax.random.normal(ks[2], (DIR_IN, DIR_K), dtype=jnp.float32) * s, 'cen2cen': jax.random.normal(ks[3], (CEN_OUT, CEN_IN), dtype=jnp.float32) * s, 'par2cen': jax.random.normal(ks[4], (CEN_OUT, DIR_IN), dtype=jnp.float32) * s, 'dia2cen': jax.random.normal(ks[5], (CEN_OUT, DIR_IN), dtype=jnp.float32) * s, 'cen2dir': jax.random.normal(ks[6], (DIR_OUT, CEN_IN), dtype=jnp.float32) * s, 'dir2dir': jax.random.normal(ks[7], (DIR_OUT, DIR_IN), dtype=jnp.float32) * s}
    _L0_conv_all = _L0_conv_setup()
    _L0_conv_in = {k: v for k, v in _L0_conv_all.items() if k in ('cen_tensor', 'dir_tensor', 'cen2cen', 'par2cen', 'dia2cen', 'cen2dir', 'dir2dir', )}
    del _L0_conv_all

    return {
        "x": x,
        "L0_conv_cen_tensor": _L0_conv_in["cen_tensor"],
        "L0_conv_dir_tensor": _L0_conv_in["dir_tensor"],
        "L0_conv_cen2cen": _L0_conv_in["cen2cen"],
        "L0_conv_par2cen": _L0_conv_in["par2cen"],
        "L0_conv_dia2cen": _L0_conv_in["dia2cen"],
        "L0_conv_cen2dir": _L0_conv_in["cen2dir"],
        "L0_conv_dir2dir": _L0_conv_in["dir2dir"],
    }

def reference(x, L0_conv_cen_tensor, L0_conv_dir_tensor, L0_conv_cen2cen, L0_conv_par2cen, L0_conv_dia2cen, L0_conv_cen2dir, L0_conv_dir2dir):
    import jax
    import jax.numpy as jnp
    def _L0_conv_ref(x, cen_tensor, dir_tensor, cen2cen, par2cen, dia2cen, cen2dir, dir2dir):
        import jax, jax.numpy as jnp
        import numpy as np
        B, H, W = (128, 48, 48)
        CEN_IN, CEN_OUT, DIR_IN, DIR_OUT, CEN_K, DIR_K = (32, 32, 24, 24, 3, 5)
        C_IN = CEN_IN + 4 * DIR_IN

        def _dwconv(x, k):
            C = x.shape[1]
            return jax.lax.conv_general_dilated(x, k[:, None], window_strides=(1, 1), padding='SAME', dimension_numbers=('NCHW', 'OIHW', 'NCHW'), feature_group_count=C)
        cen_in = cen_tensor.shape[0]
        dir_in, K = dir_tensor.shape
        xc = x[:, :cen_in]
        xh = x[:, cen_in:cen_in + dir_in]
        xv = x[:, cen_in + dir_in:cen_in + 2 * dir_in]
        xd1 = x[:, cen_in + 2 * dir_in:cen_in + 3 * dir_in]
        xd2 = x[:, cen_in + 3 * dir_in:]
        eye = jnp.eye(K, dtype=x.dtype)
        yc = _dwconv(xc, cen_tensor)
        yh = _dwconv(xh, dir_tensor[:, None, :])
        yv = _dwconv(xv, dir_tensor[:, :, None])
        yd1 = _dwconv(xd1, dir_tensor[:, :, None] * eye)
        yd2 = _dwconv(xd2, dir_tensor[:, :, None] * eye[:, ::-1])
        mix = lambda Wm, t: jnp.einsum('oc,bchw->bohw', Wm, t)
        out_cen = mix(cen2cen, yc) + mix(par2cen, yh + yv) + mix(dia2cen, yd1 + yd2)
        od_cen = mix(cen2dir, yc)
        out_dirs = [od_cen + mix(dir2dir, t) for t in (yh, yv, yd1, yd2)]
        return jnp.concatenate([out_cen] + out_dirs, axis=1)

    def _gn(v, G=32, eps=1e-5):
        B_, C_, H_, W_ = v.shape
        g = v.reshape(B_, G, C_ // G, H_, W_)
        m = jnp.mean(g, axis=(2, 3, 4), keepdims=True)
        s = jnp.var(g, axis=(2, 3, 4), keepdims=True)
        return ((g - m) / jnp.sqrt(s + eps)).reshape(v.shape)

    def _ln_c(v, eps=1e-6):
        m = jnp.mean(v, axis=1, keepdims=True)
        s = jnp.var(v, axis=1, keepdims=True)
        return (v - m) / jnp.sqrt(s + eps)

    def _ln_t(v, eps=1e-5):
        m = jnp.mean(v, axis=-1, keepdims=True)
        s = jnp.var(v, axis=-1, keepdims=True)
        return (v - m) / jnp.sqrt(s + eps)

    def _to_tokens(v):
        B_, C_, H_, W_ = v.shape
        return v.reshape(B_, C_, H_ * W_).transpose(0, 2, 1)
    def _from_tokens(t, like):
        B_, C_, H_, W_ = like.shape
        return t.transpose(0, 2, 1).reshape(B_, C_, H_, W_)

    x = x + _L0_conv_ref(_gn(x), L0_conv_cen_tensor, L0_conv_dir_tensor, L0_conv_cen2cen, L0_conv_par2cen, L0_conv_dia2cen, L0_conv_cen2dir, L0_conv_dir2dir)
    return x


_drawn_inputs = setup_inputs


def setup_inputs(seed=0):
    import zlib

    import numpy as np

    out = dict(_drawn_inputs(seed))
    spreads = {}
    factors = {}
    for name, (base, spread) in spreads.items():
        noise = np.random.default_rng([zlib.crc32(name.encode()), seed]).standard_normal(out[name].shape)
        drawn = base * np.exp(spread * noise) if base else spread * noise
        out[name] = jnp.asarray(drawn.astype(out[name].dtype))
    for name, factor in factors.items():
        out[name] = (out[name] * factor).astype(out[name].dtype)
    return out
```

```python
from contextlib import ExitStack

import concourse.bass as bass
from concourse import mybir

F32 = mybir.dt.float32
F16 = mybir.dt.float16
ALU = mybir.AluOpType
ACT = mybir.ActivationFunctionType
AX = mybir.AxisListType

P = 128
EPS = 1e-5

CEN, DIR = 32, 24
GROUP = 4
HW = 48
PIX = HW * HW

PITCH = HW + 2
BASE = 2 * (PITCH + 1) + 2
SPAN = (HW - 1) * PITCH + HW
LEN = BASE + SPAN + 3 * (PITCH + 1) + 3
LEN += LEN % 2
STEPS = [1, PITCH, PITCH + 1, PITCH - 1]

ROWS = [10, 10, 10, 10, 8]
NCH = len(ROWS)
ROW0 = [sum(ROWS[:c]) for c in range(NCH)]
CHUNK = max(ROWS) * HW

XR = 8
U = 8
NR, ER = 2, 2
YR, OR = 2, 2
NORM_AHEAD, STATS_AHEAD, LOAD_AHEAD = 2, 5, 6

DIR_VAR = [("h", 0), ("h", 1), ("h", 2), ("l", 0), ("l", 1)]
DIR_BLOCK = {"h": (0, 3), "l": (3 * DIR, 2)}
DIR_PASS = [
    (-2, [("h", 0), ("h", 1), ("h", 2), ("h", 0), ("h", 1)]),
    (1, [("h", 3), ("h", 4), None, ("h", 3), ("h", 4)]),
    (0, [("l", 2), ("l", 3), ("l", 4), ("h", 2), None]),
    (-2, [("l", 0), ("l", 1), None, None, None]),
]
CEN_VAR = [("h", -1), ("h", 0), ("h", 1), ("l", 0)]
CEN_BLOCK = {"h": (0, 3), "l": (3 * CEN, 1)}
CEN_PASS = []
for _dy in (-1, 0, 1):
    _t = 3 * (_dy + 1)
    CEN_PASS += [
        (_dy * PITCH, [("h", _t), ("h", _t + 1), ("h", _t + 2), ("h", _t + 1)]),
        (_dy * PITCH + 1, [("l", _t + 1), ("l", _t + 2), None, ("h", _t + 2)]),
        (_dy * PITCH - 1, [None, ("l", _t), None, ("h", _t)]),
    ]
PLACES = []
for _g in range(4):
    _c = 0
    while _c < DIR:
        _at = CEN + DIR * _g + _c
        _n = min(DIR - _c, 32 - _at % 32)
        PLACES.append((_g, _at // 32, _at % 32, _c, _n))
        _c += _n


def build(nc, x_in, cen_k, dir_k, cen2cen_t, par2cen_t, dia2cen_t, cen2dir_t, dir2dir_t, out):
    B = x_in.shape[0]
    n_iter = B // U
    x_d = x_in.rearrange("b c h w -> b c (h w)")
    out_d = out.rearrange("b c h w -> b c (h w)")

    ctx = ExitStack()
    with ctx:
        def sb(name, shape, dt):
            return ctx.enter_context(nc.sbuf_tensor(name, shape, dt))

        def ps(name, shape, dt):
            return ctx.enter_context(nc.psum_tensor(name, shape, dt))

        def sem(name):
            return ctx.enter_context(nc.semaphore(name))

        images = sb("images", [P, XR, PIX], F32)
        split = sb("split", [P, NR, 2, LEN], F16)
        stacked = sb("stacked", [P, ER, 5, LEN], F16)
        xn_piece = sb("xn_piece", [P, 2, CHUNK], F32)
        y_sb = sb("y_sb", [P, YR, CHUNK], F32)

        piece_stats = sb("piece_stats", [P, 4, NCH, 6], F32)
        chan_stats = sb("chan_stats", [P, 2, 2], F32)
        mean_gap = sb("mean_gap", [P, 2], F32)
        spread = sb("spread", [P, 2], F32)
        var_eps = sb("var_eps", [P, 2], F32)
        std = sb("std", [P, 2], F32)
        inv0 = sb("inv0", [P, 2], F32)
        newton = sb("newton", [P, 3, 2], F32)
        norm_scale = sb("norm_scale", [P, 4, 2], F32)
        norm_bias = sb("norm_bias", [P, 4, 2], F32)

        group_mean = sb("group_mean", [P, P], F32)
        mix_w = sb("mix_w", [P, P], F32)
        dir_sel = sb("dir_sel", [P, len(DIR_VAR), DIR], F32)
        cen_sel = sb("cen_sel", [P, len(CEN_VAR), CEN], F32)
        dir_taps = sb("dir_taps", [P, 5], F32)
        cen_taps = sb("cen_taps", [P, 9], F32)
        nat_taps = sb("nat_taps", [P, 9], F32)
        tap_max = sb("tap_max", [P, 3], F32)
        tap_inv = sb("tap_inv", [P, 3], F32)
        dir_tap16 = sb("dir_tap16", [P, 5], F16)
        cen_tap16 = sb("cen_tap16", [P, 9], F16)
        dir_part = sb("dir_part", [P, 2, 5], F32)
        cen_part = sb("cen_part", [P, 2, 9], F32)
        dir_w = sb("dir_w", [P, len(DIR_PASS), DIR], F32)
        cen_w = sb("cen_w", [P, len(CEN_PASS), CEN], F32)
        cen_w16 = sb("cen_w16", [P, len(CEN_PASS), CEN], F16)
        dir_w16 = sb("dir_w16", [P, len(PLACES), len(DIR_PASS), 32], F16)

        y_ps = ps("y_ps", [P, YR, 512], F32)
        out_ps = ps("out_ps", [P, OR, 512], F32)
        stat_ps = ps("stat_ps", [P, 512], F32)

        taps_loaded = sem("taps_loaded")
        mix_loaded = sem("mix_loaded")
        masks_made = sem("masks_made")
        pool_step = sem("pool_step")
        tables_zeroed = sem("tables_zeroed")
        padding_zeroed = sem("padding_zeroed")
        lanes_zeroed = sem("lanes_zeroed")
        stats_made = sem("stats_made")
        newton_step = sem("newton_step")
        weights_made = sem("weights_made")
        dve_step = sem("dve_step")
        loaded = [sem(f"loaded{s}") for s in range(XR)]
        stored = [sem(f"stored{s}") for s in range(XR)]
        chan_stats_made = sem("chan_stats_made")
        group_mean_made = sem("group_mean_made")
        spread_made = sem("spread_made")
        group_var_made = sem("group_var_made")
        var_eps_made = sem("var_eps_made")
        std_made = sem("std_made")
        norm_ready = sem("norm_ready")
        xn_made = sem("xn_made")
        hi_made = sem("hi_made")
        lo_made = sem("lo_made")
        stacked_loaded = [sem(f"stacked_loaded{s}") for s in range(U)]
        y_made = sem("y_made")
        y_copied = sem("y_copied")
        mixed = sem("mixed")
        added = sem("added")

        N_STACK = 4 * len(DIR_BLOCK) + 2

        def rows(ap, start, n):
            return ap[:, start:start + n * PITCH].rearrange("p (r w) -> p r w", w=PITCH)[:, :, 0:HW]

        def pixels(ap, c):
            return ap[:, ROW0[c] * HW:(ROW0[c] + ROWS[c]) * HW]

        def here(it, m):
            return not isinstance(it, int) or U * it + m < B

        def wait(eng, s, count):
            if not isinstance(count, int) or count > 0:
                eng.wait_ge(s, count)

        def run(eng, prologue, body):
            prologue()
            body(0)
            with eng.Fori(1, n_iter - 1) as it:
                body(it)
            body(n_iter - 1)

        block = ctx.enter_context(nc.Block())

        @block.sync
        def _(sp):
            def load(it, m):
                if here(it, m):
                    s = m % XR
                    if isinstance(it, int):
                        wait(sp, stored[s], 16 * (it + m // U))
                    else:
                        sp.wait_ge(stored[s], 16 * it + 16 * (m // U))
                    sp.dma_start(images[:, s, :], x_d[it * U + m, :, :]).then_inc(loaded[s], 16)

            def stack(it, m):
                if not here(it, m):
                    return
                n, e = m % NR, m % ER
                wait(sp, lo_made, NCH * U * it + NCH * (m + 1))
                done = stacked_loaded[m % U]
                for k, (first, nv) in enumerate(DIR_BLOCK.values()):
                    for g, step in enumerate(STEPS):
                        a, b = BASE - 2 * step, BASE + SPAN + step
                        src = split[CEN + DIR * g:CEN + DIR * (g + 1), n, k, a:b]
                        src = bass.AP(tensor=src.tensor, offset=src.offset,
                                      ap=[src.ap[0], [step, nv], src.ap[1]])
                        sp.dma_start(stacked[first:first + nv * DIR, e, 1 + g, a:b], src).then_inc(done, 16)
                a, b = BASE - PITCH - 1, BASE + SPAN + PITCH + 1
                src = split[0:CEN, n, 0, a - 1:b - 1]
                src = bass.AP(tensor=src.tensor, offset=src.offset, ap=[src.ap[0], [1, 3], src.ap[1]])
                sp.dma_start(stacked[0:3 * CEN, e, 0, a:b], src).then_inc(done, 16)
                sp.dma_start(stacked[3 * CEN:P, e, 0, a:b], split[0:CEN, n, 1, a:b]).then_inc(done, 16)

            def store(it, m):
                s = m % XR
                wait(sp, added, NCH * U * it + NCH * (m + 1))
                sp.dma_start(out_d[it * U + m, :, :], images[:, s, :]).then_inc(stored[s], 16)

            def prologue():
                for m in range(2):
                    load(0, m)
                sp.wait_ge(tables_zeroed, 3)
                for first, nv in DIR_BLOCK.values():
                    for v in range(nv):
                        sp.dma_start(dir_taps[first + v:first + nv * DIR:nv, :], dir_k).then_inc(taps_loaded, 16)
                for first, nv in CEN_BLOCK.values():
                    for v in range(nv):
                        sp.dma_start(cen_taps[first + v:first + nv * CEN:nv, :],
                                     cen_k.rearrange("c a b -> c (a b)")).then_inc(taps_loaded, 16)
                sp.dma_start(nat_taps[0:CEN, :], cen_k.rearrange("c a b -> c (a b)")).then_inc(taps_loaded, 16)
                for g in range(4):
                    c0 = CEN + DIR * g
                    sp.dma_start(nat_taps[c0:c0 + DIR, 0:5], dir_k).then_inc(taps_loaded, 16)
                sp.dma_start(mix_w[0:CEN, 0:CEN], cen2cen_t).then_inc(mix_loaded, 16)
                for g in range(4):
                    c0 = CEN + DIR * g
                    sp.dma_start(mix_w[0:CEN, c0:c0 + DIR], cen2dir_t).then_inc(mix_loaded, 16)
                    sp.dma_start(mix_w[c0:c0 + DIR, 0:CEN],
                                 par2cen_t if g < 2 else dia2cen_t).then_inc(mix_loaded, 16)
                    sp.dma_start(mix_w[c0:c0 + DIR, c0:c0 + DIR], dir2dir_t).then_inc(mix_loaded, 16)
                for m in range(2, LOAD_AHEAD):
                    load(0, m)
                sp.wait_ge(lanes_zeroed, 1)
                stack(0, 0)

            def body(it):
                for u in range(U):
                    stack(it, u + 1)
                    if not isinstance(it, int) or it * U + u > 0:
                        store(it, u - 1) if u else store(it - 1, U - 1)
                    load(it, u + LOAD_AHEAD)

            run(sp, prologue, body)
            store(n_iter - 1, U - 1)
            for s in range(XR):
                sp.wait_ge(stored[s], 16 * (B // XR))

        @block.gpsimd
        def _(pool):
            count = [0]

            def link(ins):
                count[0] += 1
                ins.then_inc(pool_step, 1)
                pool.wait_ge(pool_step, count[0])

            for i, table in enumerate((mix_w, nat_taps, dir_taps)):
                nc.gpsimd.memset(table[:], 0.0).then_inc(tables_zeroed, 1)
                pool.wait_ge(tables_zeroed, i + 1)
            link(nc.gpsimd.memset(dir_sel[:], 0.0))
            link(nc.gpsimd.memset(cen_sel[:], 0.0))
            link(nc.gpsimd.memset(group_mean[:], 1.0 / GROUP))
            for sel, blocks, cols in ((dir_sel, DIR_BLOCK, DIR), (cen_sel, CEN_BLOCK, CEN)):
                variants = [(first + k, nv) for first, nv in blocks.values() for k in range(nv)]
                for v, (start, nv) in enumerate(variants):
                    link(nc.gpsimd.affine_select(
                        out=sel[:, v, :], in_=sel[:, v, :], compare_op=ALU.not_equal, fill=1.0,
                        base=-start, pattern=[[-nv, cols]], channel_multiplier=1))
            gv = group_mean[:, :].rearrange("p (a b) -> p a b", b=GROUP)
            link(nc.gpsimd.affine_select(
                out=gv, in_=gv, compare_op=ALU.is_ge, fill=0.0,
                base=0, pattern=[[-GROUP, P // GROUP], [0, GROUP]], channel_multiplier=1))
            nc.gpsimd.affine_select(
                out=gv, in_=gv, compare_op=ALU.is_ge, fill=0.0,
                base=GROUP - 1, pattern=[[GROUP, P // GROUP], [0, GROUP]],
                channel_multiplier=-1).then_inc(masks_made, 1)
            pool.wait_ge(masks_made, 1)
            nc.gpsimd.memset(stacked[96:P, :, 1:5, :].bitcast(mybir.dt.uint32), 0).then_inc(lanes_zeroed, 1)

        @block.scalar
        def _(act):
            def normalise(it, m, c):
                if not here(it, m):
                    return
                s, n, pair, k = m % XR, m % NR, (m // 2) % 4, m % 2
                t = NCH * m + c
                if c == 0:
                    wait(act, norm_ready, U // 2 * it + m // 2 + 1)
                    if not isinstance(it, int) or it * U + m >= NR:
                        mm = m - NR
                        act.wait_ge(stacked_loaded[mm % U], 16 * N_STACK * (it + mm // U + 1))
                bias, scale = norm_bias[:, pair, k:k + 1], norm_scale[:, pair, k:k + 1]
                wait(act, lo_made, NCH * U * it + t + 1 - 2)
                px = pixels(images[:, s, :], c)
                nc.scalar.activation(xn_piece[:, t % 2, 0:ROWS[c] * HW], px, ACT.Identity,
                                     bias=bias, scale=scale).then_inc(xn_made, 1)
                nc.scalar.activation(rows(split[:, n, 0, :], BASE + ROW0[c] * PITCH, ROWS[c]),
                                     px.rearrange("p (r w) -> p r w", w=HW), ACT.Identity,
                                     bias=bias, scale=scale).then_inc(hi_made, 1)

            def copy_y(it, u, c):
                t = NCH * u + c
                n = ROWS[c] * HW
                act.wait_ge(y_made, NCH * U * it + t + 1)
                wait(act, mixed, NCH * U * it + t + 1 - YR)
                nc.scalar.activation(y_sb[:, t % YR, 0:n], y_ps[:, t % YR, 0:n], ACT.Identity,
                                     scale=tap_max[:, 2:3]).then_inc(y_copied, 1)

            def deviation(it, q):
                act.wait_ge(var_eps_made, U // 2 * it + q + 1)
                nc.scalar.activation(std[:, :], var_eps[:, :], ACT.Sqrt).then_inc(std_made, 1)

            def prologue():
                act.wait_ge(padding_zeroed, 1)
                deviation(0, 0)
                for c in range(NCH):
                    normalise(0, 0, c)
                deviation(0, 1)
                for c in range(NCH):
                    normalise(0, 1, c)
                act.wait_ge(weights_made, 1)

            def body(it):
                for u in range(U):
                    for c in range(NCH):
                        copy_y(it, u, c)
                        normalise(it, u + NORM_AHEAD, c)
                        if c == NCH - 1 and u % 2 and here(it, u + 3):
                            deviation(it, (u + 3) // 2)

            run(act, prologue, body)

        @block.vector
        def _(dve):
            count = [0]

            def link(ins):
                count[0] += 1
                ins.then_inc(dve_step, 1)
                dve.wait_ge(dve_step, count[0])

            def stats_piece(it, m, c):
                if not here(it, m):
                    return
                s = m % XR
                if c == 0:
                    dve.wait_ge(loaded[s], 16 * (it + m // U + 1))
                nc.vector.bn_stats(piece_stats[:, m % 4, c, :], pixels(images[:, s, :], c)).then_inc(stats_made, 1)

            def pieces_made(it, q):
                dve.wait_ge(stats_made, NCH * U * it + 2 * NCH * (q + 1))

            def channel_stats(it, q):
                for k in range(2):
                    nc.vector.bn_aggr(chan_stats[:, k, :], piece_stats[:, (2 * q + k) % 4, :, :]).then_inc(chan_stats_made, 1)

            def channel_spread(it, q):
                n = U // 2 * it + q
                means, vars_ = chan_stats[:, :, 0], chan_stats[:, :, 1]
                dve.wait_ge(group_mean_made, n + 1)
                nc.vector.tensor_tensor(mean_gap[:, :], means, stat_ps[:, 0:2], ALU.subtract).then_inc(spread_made, 1)
                dve.wait_ge(spread_made, 3 * n + 1)
                nc.vector.tensor_tensor(mean_gap[:, :], mean_gap[:, :], mean_gap[:, :], ALU.mult).then_inc(spread_made, 1)
                dve.wait_ge(spread_made, 3 * n + 2)
                nc.vector.tensor_tensor(spread[:, :], mean_gap[:, :], vars_, ALU.add).then_inc(spread_made, 1)

            def variance(it, q):
                n = U // 2 * it + q
                dve.wait_ge(group_var_made, n + 1)
                nc.vector.tensor_scalar(var_eps[:, :], stat_ps[:, 2:4], EPS, None, ALU.add).then_inc(var_eps_made, 1)

            def scale_and_bias(it, q):
                n = U // 2 * it + q
                dve.wait_ge(std_made, n + 1)
                nc.vector.reciprocal(inv0[:, :], std[:, :]).then_inc(newton_step, 1)
                dve.wait_ge(newton_step, 5 * n + 1)
                nc.vector.tensor_tensor(newton[:, 0, :], inv0[:, :], inv0[:, :], ALU.mult).then_inc(newton_step, 1)
                dve.wait_ge(newton_step, 5 * n + 2)
                nc.vector.tensor_tensor(newton[:, 1, :], newton[:, 0, :], var_eps[:, :], ALU.mult).then_inc(newton_step, 1)
                dve.wait_ge(newton_step, 5 * n + 3)
                nc.vector.tensor_scalar(newton[:, 2, :], newton[:, 1, :], -0.5, 1.5, ALU.mult, ALU.add).then_inc(newton_step, 1)
                dve.wait_ge(newton_step, 5 * n + 4)
                nc.vector.tensor_tensor(norm_scale[:, q % 4, :], newton[:, 2, :], inv0[:, :], ALU.mult).then_inc(newton_step, 1)
                dve.wait_ge(newton_step, 5 * n + 5)
                nc.vector.scalar_tensor_tensor(norm_bias[:, q % 4, :], stat_ps[:, 0:2], -1.0,
                                               norm_scale[:, q % 4, :], ALU.mult, ALU.mult).then_inc(norm_ready, 1)

            def low_part(it, m, c):
                if not here(it, m):
                    return
                n = m % NR
                t = NCH * m + c
                dve.wait_ge(hi_made, NCH * U * it + t + 1)
                at = BASE + ROW0[c] * PITCH
                nc.vector.tensor_tensor(
                    rows(split[:, n, 1, :], at, ROWS[c]),
                    xn_piece[:, t % 2, 0:ROWS[c] * HW].rearrange("p (r w) -> p r w", w=HW),
                    rows(split[:, n, 0, :], at, ROWS[c]), ALU.subtract).then_inc(lo_made, 1)

            def add_residual(it, u, c):
                t = NCH * u + c
                dve.wait_ge(mixed, NCH * U * it + t + 1)
                px = pixels(images[:, u % XR, :], c)
                nc.vector.tensor_tensor(px, out_ps[:, t % OR, 0:ROWS[c] * HW], px, ALU.add).then_inc(added, 1)

            def part_weights(taps, part, w, sel, passes, tap16, col):
                link(nc.vector.tensor_scalar(taps[:], taps[:], tap_inv[:, col:col + 1], None, ALU.mult))
                link(nc.vector.tensor_copy(tap16[:], taps[:]))
                link(nc.vector.tensor_copy(part[:, 0, :], tap16[:]))
                link(nc.vector.tensor_tensor(tap16[:], taps[:], part[:, 0, :], ALU.subtract))
                link(nc.vector.tensor_copy(part[:, 1, :], tap16[:]))
                link(nc.vector.memset(w[:], 0.0))
                for p, (_, uses) in enumerate(passes):
                    for v, use in enumerate(uses):
                        if use is not None:
                            k = part[:, "hl".index(use[0]), use[1]:use[1] + 1]
                            link(nc.vector.scalar_tensor_tensor(w[:, p, :], sel[:, v, :], k, w[:, p, :],
                                                                ALU.mult, ALU.add))

            def make_weights():
                dve.wait_ge(taps_loaded, 16 * (len(DIR_VAR) + len(CEN_VAR) + 5))
                dve.wait_ge(masks_made, 1)
                for col, taps in enumerate((dir_taps, cen_taps, nat_taps)):
                    link(nc.vector.tensor_reduce(tap_max[:, col:col + 1], taps[:], AX.X, ALU.max,
                                                 apply_absolute_value=True))
                link(nc.vector.tensor_scalar(tap_max[:, :], tap_max[:, :], 1e-30, None, ALU.max))
                link(nc.vector.reciprocal(tap_inv[:, :], tap_max[:, :]))
                part_weights(dir_taps, dir_part, dir_w, dir_sel, DIR_PASS, dir_tap16, 0)
                part_weights(cen_taps, cen_part, cen_w, cen_sel, CEN_PASS, cen_tap16, 1)
                link(nc.vector.memset(dir_w16[:], 0.0))
                for i, (g, q, col, ch, n) in enumerate(PLACES):
                    nc.vector.tensor_copy(dir_w16[:, i, :, col:col + n], dir_w[:, :, ch:ch + n])
                link(nc.vector.tensor_copy(cen_w16[:], cen_w[:]))
                nc.vector.tensor_copy(tap_inv[:, 0:1], tap_max[:, 2:3]).then_inc(weights_made, 1)

            def prologue():
                nc.vector.memset(split[:].bitcast(mybir.dt.uint32), 0).then_inc(padding_zeroed, 1)
                for m in range(2):
                    for c in range(NCH):
                        stats_piece(0, m, c)
                dve.wait_ge(masks_made, 1)
                pieces_made(0, 0)
                channel_stats(0, 0)
                channel_spread(0, 0)
                variance(0, 0)
                scale_and_bias(0, 0)
                for c in range(NCH):
                    low_part(0, 0, c)
                for m in range(2, 4):
                    for c in range(NCH):
                        stats_piece(0, m, c)
                pieces_made(0, 1)
                channel_stats(0, 1)
                channel_spread(0, 1)
                variance(0, 1)
                scale_and_bias(0, 1)
                make_weights()
                for c in range(NCH):
                    low_part(0, 1, c)
                for c in range(NCH):
                    stats_piece(0, 4, c)

            def body(it):
                for u in range(U):
                    for c in range(NCH):
                        pair = u % 2 and here(it, u + 3)
                        q = (u + 3) // 2
                        if pair and c == 0:
                            pieces_made(it, q)
                        add_residual(it, u, c)
                        if pair and c == 0:
                            channel_stats(it, q)
                        low_part(it, u + NORM_AHEAD, c)
                        stats_piece(it, u + STATS_AHEAD, c)
                        if pair and c == 1:
                            channel_spread(it, q)
                        if pair and c == 3:
                            variance(it, q)
                        if pair and c == 4:
                            scale_and_bias(it, q)

            run(dve, prologue, body)

        @block.tensor
        def _(pe):
            passes = [[] for _ in range(4)]
            for p, (off, _) in enumerate(CEN_PASS):
                passes[0].append((0, off, cen_w16[:, p, :]))
            for i, (g, q, _, _, _) in enumerate(PLACES):
                for p, (off, _) in enumerate(DIR_PASS):
                    passes[q].append((1 + g, off * STEPS[g], dir_w16[:, i, p, :]))

            def depthwise(it, m, c):
                if not here(it, m):
                    return
                e = m % ER
                t = NCH * m + c
                if c == 0:
                    pe.wait_ge(stacked_loaded[m % U], 16 * N_STACK * (it + m // U + 1))
                wait(pe, y_copied, NCH * U * it + t + 1 - YR)
                for r in range(max(len(x) for x in passes)):
                    for q in range(4):
                        if r < len(passes[q]):
                            tile, off, w = passes[q][r]
                            mm = nc.tensor.matmul(
                                y_ps[32 * q:32 * (q + 1), t % YR, 0:ROWS[c] * HW], w,
                                rows(stacked[:, e, tile, :], BASE + off + ROW0[c] * PITCH, ROWS[c]),
                                start=(r == 0), stop=(r == len(passes[q]) - 1))
                mm.then_inc(y_made, 1)

            def mix(it, u, c):
                t = NCH * u + c
                n = ROWS[c] * HW
                pe.wait_ge(y_copied, NCH * U * it + t + 1)
                wait(pe, added, NCH * U * it + t + 1 - OR)
                nc.tensor.matmul(out_ps[:, t % OR, 0:n], mix_w[:, :], y_sb[:, t % YR, 0:n],
                                 start=True, stop=True).then_inc(mixed, 1)

            def means(it, q):
                pe.wait_ge(chan_stats_made, U * it + 2 * q + 2)
                nc.tensor.matmul(stat_ps[:, 0:2], group_mean[:, :], chan_stats[:, :, 0],
                                 start=True, stop=True).then_inc(group_mean_made, 1)

            def variances(it, q):
                pe.wait_ge(spread_made, 3 * (U // 2) * it + 3 * q + 3)
                nc.tensor.matmul(stat_ps[:, 2:4], group_mean[:, :], spread[:, :],
                                 start=True, stop=True).then_inc(group_var_made, 1)

            def prologue():
                pe.wait_ge(masks_made, 1)
                for q in range(2):
                    means(0, q)
                    variances(0, q)
                pe.wait_ge(mix_loaded, 16 * 13)
                pe.wait_ge(weights_made, 1)
                depthwise(0, 0, 0)

            def body(it):
                for u in range(U):
                    pair = u % 2 and here(it, u + 3)
                    q = (u + 3) // 2
                    for c in range(NCH):
                        if c < NCH - 1:
                            depthwise(it, u, c + 1)
                        else:
                            depthwise(it, u + 1, 0)
                        mix(it, u, c)
                        if pair and c == 0:
                            means(it, q)
                        if pair and c == 2:
                            variances(it, q)

            run(pe, prologue, body)


_INS = ["x", "L0_conv_cen_tensor", "L0_conv_dir_tensor", "L0_conv_cen2cen", "L0_conv_par2cen",
        "L0_conv_dia2cen", "L0_conv_cen2dir", "L0_conv_dir2dir"]


def kernel(**inputs):
    import numpy as np
    import concourse.bacc as bacc
    from concourse.bass_utils import run_bass_kernel_spmd

    nc = bacc.Bacc("TRN2", target_bir_lowering=False, num_devices=1)
    arrays, args = {}, []
    for i, name in enumerate(_INS):
        a = np.asarray(inputs[name])
        if i >= 3:
            a = a.T
        a = np.ascontiguousarray(a)
        arrays[f"in_{name}"] = a
        args.append(nc.dram_tensor(f"in_{name}", a.shape, mybir.dt.from_np(a.dtype), kind="ExternalInput").ap())
    x = inputs["x"]
    args.append(nc.dram_tensor("out_0", tuple(x.shape), F32, kind="ExternalOutput").ap())
    build(nc, *args)
    r = run_bass_kernel_spmd(nc, [arrays], core_ids=[0])
    return r.results[0]["out_0"]
```

```python
from contextlib import ExitStack

import concourse.bass as bass
from concourse import mybir

F32 = mybir.dt.float32
F16 = mybir.dt.float16
ALU = mybir.AluOpType
ACT = mybir.ActivationFunctionType
AX = mybir.AxisListType

P = 128
EPS = 1e-5

CEN, DIR = 32, 24
GROUP = 4
HW = 48
PIX = HW * HW

PITCH = HW + 2
BASE = 2 * (PITCH + 1) + 2
SPAN = (HW - 1) * PITCH + HW
LEN = BASE + SPAN + 3 * (PITCH + 1) + 3
LEN += LEN % 2
STEPS = [1, PITCH, PITCH + 1, PITCH - 1]

ROWS = [10, 10, 10, 10, 8]
NCH = len(ROWS)
ROW0 = [sum(ROWS[:c]) for c in range(NCH)]
CHUNK = max(ROWS) * HW

XR = 8
U = 8
NR, ER = 2, 2
YR, OR = 2, 2
NORM_AHEAD, STATS_AHEAD, LOAD_AHEAD = 2, 5, 6

DIR_VAR = [("h", 0), ("h", 1), ("h", 2), ("l", 0), ("l", 1)]
DIR_BLOCK = {"h": (0, 3), "l": (3 * DIR, 2)}
DIR_PASS = [
    (-2, [("h", 0), ("h", 1), ("h", 2), ("h", 0), ("h", 1)]),
    (1, [("h", 3), ("h", 4), None, ("h", 3), ("h", 4)]),
    (0, [("l", 2), ("l", 3), ("l", 4), ("h", 2), None]),
    (-2, [("l", 0), ("l", 1), None, None, None]),
]
CEN_VAR = [("h", -1), ("h", 1), ("h", 0), ("l", 0)]
CEN_PASS = []
for _dy in (-1, 0, 1):
    _t = 3 * (_dy + 1)
    CEN_PASS += [
        (_dy * PITCH, [("h", _t), ("h", _t + 2), ("h", _t + 1), ("h", _t + 1)]),
        (_dy * PITCH + 1, [("l", _t + 1), None, ("l", _t + 2), ("h", _t + 2)]),
        (_dy * PITCH - 1, [None, None, ("l", _t), ("h", _t)]),
    ]
Y_SCALE = 16.0

PLACES = []
for _g in range(4):
    _c = 0
    while _c < DIR:
        _at = CEN + DIR * _g + _c
        _n = min(DIR - _c, 32 - _at % 32)
        PLACES.append((_g, _at // 32, _at % 32, _c, _n))
        _c += _n


def build(nc, x_in, cen_k, dir_k, cen2cen_t, par2cen_t, dia2cen_t, cen2dir_t, dir2dir_t, out):
    B = x_in.shape[0]
    n_iter = B // U
    x_d = x_in.rearrange("b c h w -> b c (h w)")
    out_d = out.rearrange("b c h w -> b c (h w)")

    ctx = ExitStack()
    with ctx:
        def sb(name, shape, dt):
            return ctx.enter_context(nc.sbuf_tensor(name, shape, dt))

        def ps(name, shape, dt):
            return ctx.enter_context(nc.psum_tensor(name, shape, dt))

        def sem(name):
            return ctx.enter_context(nc.semaphore(name))

        images = sb("images", [P, XR, PIX], F32)
        split = sb("split", [P, NR, 2, LEN], F16)
        stacked = sb("stacked", [P, ER, 5, LEN], F16)
        xn_piece = sb("xn_piece", [P, 2, CHUNK], F32)
        y_sb = sb("y_sb", [P, YR, 2, CHUNK], F16)

        piece_stats = sb("piece_stats", [P, 4, NCH, 6], F32)
        chan_stats = sb("chan_stats", [P, 2, 2], F32)
        mean_gap = sb("mean_gap", [P, 2], F32)
        spread = sb("spread", [P, 2], F32)
        var_eps = sb("var_eps", [P, 2], F32)
        std = sb("std", [P, 2], F32)
        inv0 = sb("inv0", [P, 2], F32)
        newton = sb("newton", [P, 3, 2], F32)
        norm_scale = sb("norm_scale", [P, 4, 2], F32)
        norm_bias = sb("norm_bias", [P, 4, 2], F32)

        group_mean = sb("group_mean", [P, P], F32)
        mix_w = sb("mix_w", [P, P], F32)
        mix_hi32 = sb("mix_hi32", [P, P], F32)
        mix_w16 = sb("mix_w16", [P, 2, P], F16)
        dir_sel = sb("dir_sel", [P, len(DIR_VAR), DIR], F32)
        cen_sel = sb("cen_sel", [P, len(CEN_VAR), CEN], F32)
        dir_taps = sb("dir_taps", [P, 5], F32)
        cen_taps = sb("cen_taps", [P, 9], F32)
        nat_taps = sb("nat_taps", [P, 9], F32)
        row_max = sb("row_max", [P, 4], F32)
        row_inv = sb("row_inv", [P, 4], F32)
        y_scale = sb("y_scale", [P, 1], F32)
        dir_tap16 = sb("dir_tap16", [P, 2, 5], F16)
        cen_tap16 = sb("cen_tap16", [P, 2, 9], F16)
        dir_part = sb("dir_part", [P, 2, 5], F32)
        cen_part = sb("cen_part", [P, 2, 9], F32)
        dir_lane = sb("dir_lane", [P, len(DIR_VAR)], F32)
        cen_lane = sb("cen_lane", [P, len(CEN_VAR)], F32)
        dir_diag = sb("dir_diag", [P, DIR], F32)
        cen_diag = sb("cen_diag", [P, CEN], F32)
        dir_coef = sb("dir_coef", [P, len(DIR_PASS)], F32)
        cen_coef = sb("cen_coef", [P, len(CEN_PASS)], F32)
        dir_w = sb("dir_w", [P, len(DIR_PASS), DIR], F32)
        cen_w16 = sb("cen_w16", [P, len(CEN_PASS), CEN], F16)
        dir_w16 = sb("dir_w16", [P, len(PLACES), len(DIR_PASS), 32], F16)

        y_ps = ps("y_ps", [P, YR, 512], F32)
        out_ps = ps("out_ps", [P, OR, 512], F32)
        stat_ps = ps("stat_ps", [P, 512], F32)

        taps_loaded = sem("taps_loaded")
        mix_loaded = sem("mix_loaded")
        masks_made = sem("masks_made")
        pool_step = sem("pool_step")
        tables_zeroed = sem("tables_zeroed")
        padding_zeroed = sem("padding_zeroed")
        lanes_zeroed = sem("lanes_zeroed")
        stats_made = sem("stats_made")
        newton_step = sem("newton_step")
        weights_made = sem("weights_made")
        dve_step = sem("dve_step")
        loaded = [sem(f"loaded{s}") for s in range(XR)]
        stored = [sem(f"stored{s}") for s in range(XR)]
        chan_stats_made = sem("chan_stats_made")
        group_mean_made = sem("group_mean_made")
        spread_made = sem("spread_made")
        group_var_made = sem("group_var_made")
        var_eps_made = sem("var_eps_made")
        std_made = sem("std_made")
        norm_ready = sem("norm_ready")
        xn_made = sem("xn_made")
        hi_made = sem("hi_made")
        lo_made = sem("lo_made")
        stacked_loaded = [sem(f"stacked_loaded{s}") for s in range(U)]
        y_made = sem("y_made")
        y_hi_made = sem("y_hi_made")
        y_lo_made = sem("y_lo_made")
        centre_stacked = sem("centre_stacked")
        centre_zeroed = sem("centre_zeroed")
        pool_tick = sem("pool_tick")
        mixed = sem("mixed")
        added = sem("added")

        N_STACK = 4 * len(DIR_BLOCK) + 2

        N_CEN = NCH * 2

        def rows(ap, start, n):
            return ap[:, start:start + n * PITCH].rearrange("p (r w) -> p r w", w=PITCH)[:, :, 0:HW]

        def pixels(ap, c):
            return ap[:, ROW0[c] * HW:(ROW0[c] + ROWS[c]) * HW]

        def here(it, m):
            return not isinstance(it, int) or U * it + m < B

        def wait(eng, s, count):
            if not isinstance(count, int) or count > 0:
                eng.wait_ge(s, count)

        def run(eng, prologue, body):
            prologue()
            body(0)
            with eng.Fori(1, n_iter - 1) as it:
                body(it)
            body(n_iter - 1)

        block = ctx.enter_context(nc.Block())

        @block.sync
        def _(sp):
            def load(it, m):
                if here(it, m):
                    s = m % XR
                    if isinstance(it, int):
                        wait(sp, stored[s], 16 * (it + m // U))
                    else:
                        sp.wait_ge(stored[s], 16 * it + 16 * (m // U))
                    sp.dma_start(images[:, s, :], x_d[it * U + m, :, :]).then_inc(loaded[s], 16)

            def stack(it, m):
                if not here(it, m):
                    return
                n, e = m % NR, m % ER
                wait(sp, lo_made, NCH * U * it + NCH * (m + 1))
                done = stacked_loaded[m % U]
                for k, (first, nv) in enumerate(DIR_BLOCK.values()):
                    for g, step in enumerate(STEPS):
                        a, b = BASE - 2 * step, BASE + SPAN + step
                        src = split[CEN + DIR * g:CEN + DIR * (g + 1), n, k, a:b]
                        src = bass.AP(tensor=src.tensor, offset=src.offset,
                                      ap=[src.ap[0], [step, nv], src.ap[1]])
                        sp.dma_start(stacked[first:first + nv * DIR, e, 1 + g, a:b], src).then_inc(done, 16)
                a, b = BASE - PITCH - 1, BASE + SPAN + PITCH + 1
                for v in range(2):
                    shift = CEN_VAR[v][1]
                    sp.dma_start(stacked[CEN * v:CEN * (v + 1), e, 0, a:b],
                                 split[0:CEN, n, 0, a + shift:b + shift]).then_inc(done, 16)

            def store(it, m):
                s = m % XR
                wait(sp, added, NCH * U * it + NCH * (m + 1))
                sp.dma_start(out_d[it * U + m, :, :], images[:, s, :]).then_inc(stored[s], 16)

            def repeated(src, n):
                return bass.AP(tensor=src.tensor, offset=src.offset, ap=[[0, n]] + list(src.ap))

            def prologue():
                load(0, 0)
                sp.wait_ge(tables_zeroed, 3)
                for first, nv in DIR_BLOCK.values():
                    src = bass.AP(tensor=dir_k.tensor, offset=dir_k.offset, ap=[dir_k.ap[0], [0, nv], dir_k.ap[1]])
                    sp.dma_start(dir_taps[first:first + nv * DIR, :], src).then_inc(taps_loaded, 16)
                cen_k2 = cen_k.rearrange("c a b -> c (a b)")
                sp.dma_start(cen_taps[:, :], repeated(cen_k2, len(CEN_VAR))).then_inc(taps_loaded, 16)
                sp.dma_start(nat_taps[0:CEN, :], cen_k2).then_inc(taps_loaded, 16)
                sp.dma_start(nat_taps[CEN:P, 0:5], repeated(dir_k, 4)).then_inc(taps_loaded, 16)
                load(0, 1)
                sp.dma_start(mix_w[0:CEN, 0:CEN], cen2cen_t).then_inc(mix_loaded, 16)
                src = bass.AP(tensor=cen2dir_t.tensor, offset=cen2dir_t.offset,
                              ap=[cen2dir_t.ap[0], [0, 4], cen2dir_t.ap[1]])
                sp.dma_start(mix_w[0:CEN, CEN:P].rearrange("c (g d) -> c g d", g=4), src).then_inc(mix_loaded, 16)
                sp.dma_start(mix_w[CEN:CEN + 2 * DIR, 0:CEN], repeated(par2cen_t, 2)).then_inc(mix_loaded, 16)
                sp.dma_start(mix_w[CEN + 2 * DIR:P, 0:CEN], repeated(dia2cen_t, 2)).then_inc(mix_loaded, 16)
                for g in range(4):
                    c0 = CEN + DIR * g
                    sp.dma_start(mix_w[c0:c0 + DIR, c0:c0 + DIR], dir2dir_t).then_inc(mix_loaded, 16)
                load(0, 2)
                load(0, 3)
                sp.wait_ge(lanes_zeroed, 1)
                stack(0, 0)
                load(0, 4)
                load(0, 5)

            def body(it):
                for u in range(U):
                    stack(it, u + 1)
                    if not isinstance(it, int) or it * U + u > 0:
                        store(it, u - 1) if u else store(it - 1, U - 1)
                    load(it, u + LOAD_AHEAD)

            run(sp, prologue, body)
            store(n_iter - 1, U - 1)
            for s in range(XR):
                sp.wait_ge(stored[s], 16 * (B // XR))

        @block.gpsimd
        def _(pool):
            count = [0]

            def link(ins):
                count[0] += 1
                ins.then_inc(pool_step, 1)
                pool.wait_ge(pool_step, count[0])

            for i, table in enumerate((mix_w, nat_taps, dir_taps)):
                nc.gpsimd.memset(table[:], 0.0).then_inc(tables_zeroed, 1)
                pool.wait_ge(tables_zeroed, i + 1)
            link(nc.gpsimd.memset(dir_sel[:], 0.0))
            link(nc.gpsimd.memset(cen_sel[:], 0.0))
            link(nc.gpsimd.memset(group_mean[:], 1.0 / GROUP))
            dir_start = [(first + k, nv) for first, nv in DIR_BLOCK.values() for k in range(nv)]
            cen_start = [(CEN * v, 1) for v in range(len(CEN_VAR))]
            for sel, starts, cols in ((dir_sel, dir_start, DIR), (cen_sel, cen_start, CEN)):
                for v, (start, nv) in enumerate(starts):
                    link(nc.gpsimd.affine_select(
                        out=sel[:, v, :], in_=sel[:, v, :], compare_op=ALU.not_equal, fill=1.0,
                        base=-start, pattern=[[-nv, cols]], channel_multiplier=1))
            gv = group_mean[:, :].rearrange("p (a b) -> p a b", b=GROUP)
            link(nc.gpsimd.affine_select(
                out=gv, in_=gv, compare_op=ALU.is_ge, fill=0.0,
                base=0, pattern=[[-GROUP, P // GROUP], [0, GROUP]], channel_multiplier=1))
            nc.gpsimd.affine_select(
                out=gv, in_=gv, compare_op=ALU.is_ge, fill=0.0,
                base=GROUP - 1, pattern=[[GROUP, P // GROUP], [0, GROUP]],
                channel_multiplier=-1).then_inc(masks_made, 1)
            pool.wait_ge(masks_made, 1)
            nc.gpsimd.memset(stacked[96:P, :, 1:5, :].bitcast(mybir.dt.uint32), 0).then_inc(lanes_zeroed, 1)
            pool.wait_ge(lanes_zeroed, 1)
            nc.gpsimd.memset(stacked[2 * CEN:P, :, 0, :].bitcast(mybir.dt.uint32), 0).then_inc(centre_zeroed, 1)
            pool.wait_ge(centre_zeroed, 1)

            def stack_centre(it, m):
                if not here(it, m):
                    return
                n, e = m % NR, m % ER
                wait(pool, lo_made, NCH * U * it + NCH * (m + 1))
                pool.sem_inc(pool_tick, 1)
                for c in range(NCH):
                    a = BASE + ROW0[c] * PITCH
                    b = a + ROWS[c] * PITCH
                    for v, (part, shift) in enumerate(CEN_VAR):
                        if shift == 0:
                            nc.gpsimd.tensor_copy(
                                stacked[CEN * v:CEN * (v + 1), e, 0, a:b].bitcast(mybir.dt.uint32),
                                split[0:CEN, n, "hl".index(part), a:b].bitcast(mybir.dt.uint32)
                            ).then_inc(centre_stacked, 1)

            def body(it):
                for u in range(U):
                    stack_centre(it, u + 1)

            run(pool, lambda: stack_centre(0, 0), body)

        @block.scalar
        def _(act):
            def normalise(it, m, c):
                if not here(it, m):
                    return
                s, n, pair, k = m % XR, m % NR, (m // 2) % 4, m % 2
                t = NCH * m + c
                if c == 0:
                    wait(act, norm_ready, U // 2 * it + m // 2 + 1)
                    if not isinstance(it, int) or it * U + m >= NR:
                        mm = m - NR
                        act.wait_ge(stacked_loaded[mm % U], 16 * N_STACK * (it + mm // U + 1))
                        act.wait_ge(centre_stacked, N_CEN * (U * it + mm + 1))
                bias, scale = norm_bias[:, pair, k:k + 1], norm_scale[:, pair, k:k + 1]
                wait(act, lo_made, NCH * U * it + t + 1 - 2)
                px = pixels(images[:, s, :], c)
                nc.scalar.activation(xn_piece[:, t % 2, 0:ROWS[c] * HW], px, ACT.Identity,
                                     bias=bias, scale=scale).then_inc(xn_made, 1)
                nc.scalar.activation(rows(split[:, n, 0, :], BASE + ROW0[c] * PITCH, ROWS[c]),
                                     px.rearrange("p (r w) -> p r w", w=HW), ACT.Identity,
                                     bias=bias, scale=scale).then_inc(hi_made, 1)

            def y_hi(it, u, c):
                t = NCH * u + c
                n = ROWS[c] * HW
                wait(act, mixed, NCH * U * it + t + 1 - YR)
                act.wait_ge(y_made, NCH * U * it + t + 1)
                nc.scalar.activation(y_sb[:, t % YR, 0, 0:n], y_ps[:, t % YR, 0:n], ACT.Identity,
                                     scale=y_scale[:, 0:1]).then_inc(y_hi_made, 1)

            def deviation(it, q):
                act.wait_ge(var_eps_made, U // 2 * it + q + 1)
                nc.scalar.activation(std[:, :], var_eps[:, :], ACT.Sqrt).then_inc(std_made, 1)

            def prologue():
                act.wait_ge(padding_zeroed, 1)
                deviation(0, 0)
                for m in range(2):
                    for c in range(NCH):
                        normalise(0, m, c)
                deviation(0, 1)
                act.wait_ge(weights_made, 1)

            def body(it):
                for u in range(U):
                    for c in range(NCH):
                        y_hi(it, u, c)
                        normalise(it, u + NORM_AHEAD, c)
                        if c == NCH - 1 and u % 2 and here(it, u + 3):
                            deviation(it, (u + 3) // 2)

            run(act, prologue, body)

        @block.vector
        def _(dve):
            count = [0]

            def link(ins):
                count[0] += 1
                ins.then_inc(dve_step, 1)
                dve.wait_ge(dve_step, count[0])

            def stats_piece(it, m, c):
                if not here(it, m):
                    return
                s = m % XR
                if c == 0:
                    dve.wait_ge(loaded[s], 16 * (it + m // U + 1))
                nc.vector.bn_stats(piece_stats[:, m % 4, c, :], pixels(images[:, s, :], c)).then_inc(stats_made, 1)

            def pieces_made(it, q):
                dve.wait_ge(stats_made, NCH * U * it + 2 * NCH * (q + 1))

            def channel_stats(it, q):
                for k in range(2):
                    nc.vector.bn_aggr(chan_stats[:, k, :], piece_stats[:, (2 * q + k) % 4, :, :]).then_inc(chan_stats_made, 1)

            def channel_spread(it, q):
                n = U // 2 * it + q
                means, vars_ = chan_stats[:, :, 0], chan_stats[:, :, 1]
                dve.wait_ge(group_mean_made, n + 1)
                nc.vector.tensor_tensor(mean_gap[:, :], means, stat_ps[:, 0:2], ALU.subtract).then_inc(spread_made, 1)
                dve.wait_ge(spread_made, 3 * n + 1)
                nc.vector.tensor_tensor(mean_gap[:, :], mean_gap[:, :], mean_gap[:, :], ALU.mult).then_inc(spread_made, 1)
                dve.wait_ge(spread_made, 3 * n + 2)
                nc.vector.tensor_tensor(spread[:, :], mean_gap[:, :], vars_, ALU.add).then_inc(spread_made, 1)

            def variance(it, q):
                n = U // 2 * it + q
                dve.wait_ge(group_var_made, n + 1)
                nc.vector.tensor_scalar(var_eps[:, :], stat_ps[:, 2:4], EPS, None, ALU.add).then_inc(var_eps_made, 1)

            def scale_and_bias(it, q):
                n = U // 2 * it + q
                dve.wait_ge(std_made, n + 1)
                nc.vector.reciprocal(inv0[:, :], std[:, :]).then_inc(newton_step, 1)
                dve.wait_ge(newton_step, 5 * n + 1)
                nc.vector.tensor_tensor(newton[:, 0, :], inv0[:, :], inv0[:, :], ALU.mult).then_inc(newton_step, 1)
                dve.wait_ge(newton_step, 5 * n + 2)
                nc.vector.tensor_tensor(newton[:, 1, :], newton[:, 0, :], var_eps[:, :], ALU.mult).then_inc(newton_step, 1)
                dve.wait_ge(newton_step, 5 * n + 3)
                nc.vector.tensor_scalar(newton[:, 2, :], newton[:, 1, :], -0.5, 1.5, ALU.mult, ALU.add).then_inc(newton_step, 1)
                dve.wait_ge(newton_step, 5 * n + 4)
                nc.vector.tensor_tensor(norm_scale[:, q % 4, :], newton[:, 2, :], inv0[:, :], ALU.mult).then_inc(newton_step, 1)
                dve.wait_ge(newton_step, 5 * n + 5)
                nc.vector.scalar_tensor_tensor(norm_bias[:, q % 4, :], stat_ps[:, 0:2], -1.0,
                                               norm_scale[:, q % 4, :], ALU.mult, ALU.mult).then_inc(norm_ready, 1)

            def low_part(it, m, c):
                if not here(it, m):
                    return
                n = m % NR
                t = NCH * m + c
                dve.wait_ge(hi_made, NCH * U * it + t + 1)
                at = BASE + ROW0[c] * PITCH
                nc.vector.tensor_tensor(
                    rows(split[:, n, 1, :], at, ROWS[c]),
                    xn_piece[:, t % 2, 0:ROWS[c] * HW].rearrange("p (r w) -> p r w", w=HW),
                    rows(split[:, n, 0, :], at, ROWS[c]), ALU.subtract).then_inc(lo_made, 1)

            def y_lo(it, u, c):
                t = NCH * u + c
                n = ROWS[c] * HW
                dve.wait_ge(y_hi_made, NCH * U * it + t + 1)
                nc.vector.scalar_tensor_tensor(y_sb[:, t % YR, 1, 0:n], y_ps[:, t % YR, 0:n], y_scale[:, 0:1],
                                               y_sb[:, t % YR, 0, 0:n], ALU.mult, ALU.subtract).then_inc(y_lo_made, 1)

            def add_residual(it, u, c):
                t = NCH * u + c
                dve.wait_ge(mixed, NCH * U * it + t + 1)
                px = pixels(images[:, u % XR, :], c)
                nc.vector.scalar_tensor_tensor(px, out_ps[:, t % OR, 0:ROWS[c] * HW], 1.0 / Y_SCALE, px,
                                               ALU.mult, ALU.add).then_inc(added, 1)

            def part_taps(pairs):
                for taps, _, _, inv in pairs:
                    last = nc.vector.tensor_scalar(taps[:], taps[:], inv, None, ALU.mult)
                link(last)
                for taps, _, tap16, _ in pairs:
                    last = nc.vector.tensor_copy(tap16[:, 0, :], taps[:])
                link(last)
                for taps, part, tap16, _ in pairs:
                    last = nc.vector.tensor_copy(part[:, 0, :], tap16[:, 0, :])
                link(last)
                for taps, part, tap16, _ in pairs:
                    last = nc.vector.tensor_tensor(tap16[:, 1, :], taps[:], part[:, 0, :], ALU.subtract)
                link(last)
                for taps, part, tap16, _ in pairs:
                    last = nc.vector.tensor_copy(part[:, 1, :], tap16[:, 1, :])
                link(last)

            def uses_of(passes, v):
                todo = [(p, *uses[v]) for p, (_, uses) in enumerate(passes) if uses[v] is not None]
                while todo:
                    same = [x for x in todo if x[1] == todo[0][1]]
                    run_ = same[:2]
                    for x in same[2:]:
                        if (x[0] - run_[-1][0], x[2] - run_[-1][2]) == (run_[1][0] - run_[0][0], run_[1][2] - run_[0][2]):
                            run_.append(x)
                    todo = [x for x in todo if x not in run_]
                    yield [x[0] for x in run_], run_[0][1], [x[2] for x in run_]

            def evenly(ap, at):
                step = at[1] - at[0] if len(at) > 1 else 1
                first = ap[:, at[0]:at[0] + 1]
                return bass.AP(tensor=first.tensor, offset=first.offset, ap=[first.ap[0], [step, len(at)]])

            def coefficients(coef, part, lane, passes, variants):
                for v in range(len(variants)):
                    for at, kind, taps in uses_of(passes, v):
                        out_ = evenly(coef[:, :], at)
                        link(nc.vector.scalar_tensor_tensor(
                            out_, evenly(part[:, "hl".index(kind), :], taps), lane[:, v:v + 1], out_,
                            ALU.mult, ALU.add))

            def make_weights():
                dve.wait_ge(taps_loaded, 16 * 5)
                dve.wait_ge(mix_loaded, 16 * 8)
                dve.wait_ge(masks_made, 1)
                for col, table in enumerate((dir_taps, cen_taps, nat_taps, mix_w)):
                    last = nc.vector.tensor_reduce(row_max[:, col:col + 1], table[:], AX.X, ALU.max,
                                                   apply_absolute_value=True)
                nc.vector.tensor_reduce(dir_lane[:, :], dir_sel[:], AX.X, ALU.add)
                nc.vector.tensor_reduce(cen_lane[:, :], cen_sel[:], AX.X, ALU.add)
                nc.vector.tensor_reduce(dir_diag[:, :], dir_sel[:].rearrange("p v c -> p c v"), AX.X, ALU.add)
                nc.vector.tensor_reduce(cen_diag[:, :], cen_sel[:].rearrange("p v c -> p c v"), AX.X, ALU.add)
                nc.vector.memset(dir_coef[:], 0.0)
                nc.vector.memset(cen_coef[:], 0.0)
                link(nc.vector.memset(dir_w16[:], 0.0))
                link(nc.vector.tensor_scalar(row_max[:, :], row_max[:, :], 1e-30, None, ALU.max))
                nc.vector.scalar_tensor_tensor(y_scale[:, :], row_max[:, 2:3], Y_SCALE, row_max[:, 3:4],
                                               ALU.mult, ALU.mult)
                link(nc.vector.reciprocal(row_inv[:, :], row_max[:, :]))
                link(nc.vector.tensor_scalar(mix_w[:], mix_w[:], row_inv[:, 3:4], None, ALU.mult))
                link(nc.vector.tensor_copy(mix_w16[:, 0, :], mix_w[:]))
                link(nc.vector.tensor_copy(mix_hi32[:], mix_w16[:, 0, :]))
                nc.vector.tensor_tensor(mix_w16[:, 1, :], mix_w[:], mix_hi32[:], ALU.subtract)
                part_taps([(dir_taps, dir_part, dir_tap16, row_inv[:, 0:1]),
                           (cen_taps, cen_part, cen_tap16, row_inv[:, 1:2])])
                coefficients(dir_coef, dir_part, dir_lane, DIR_PASS, DIR_VAR)
                coefficients(cen_coef, cen_part, cen_lane, CEN_PASS, CEN_VAR)
                for w, diag, coef, passes, cols in ((dir_w, dir_diag, dir_coef, DIR_PASS, DIR),
                                                    (cen_w16, cen_diag, cen_coef, CEN_PASS, CEN)):
                    n = len(passes)
                    d, k = diag[:, :], coef[:, :]
                    last = nc.vector.tensor_tensor(
                        w[:], bass.AP(tensor=d.tensor, offset=d.offset, ap=[d.ap[0], [0, n], [1, cols]]),
                        bass.AP(tensor=k.tensor, offset=k.offset, ap=[k.ap[0], [1, n], [0, cols]]), ALU.mult)
                link(last)
                for i, (g, q, col, ch, n) in enumerate(PLACES):
                    last = nc.vector.tensor_copy(dir_w16[:, i, :, col:col + n], dir_w[:, :, ch:ch + n])
                last.then_inc(weights_made, 1)

            def prologue():
                nc.vector.memset(split[:, :, :, 0:BASE], 0.0)
                nc.vector.memset(split[:, :, :, BASE + SPAN:LEN], 0.0)
                for n in range(NR):
                    gaps = split[:, n, :, BASE + HW:BASE + HW + PITCH * (HW - 1)]
                    last = nc.vector.memset(gaps.rearrange("p k (r w) -> p k r w", w=PITCH)[:, :, :, 0:2], 0.0)
                last.then_inc(padding_zeroed, 1)
                for m in range(2):
                    for c in range(NCH):
                        stats_piece(0, m, c)
                dve.wait_ge(masks_made, 1)
                pieces_made(0, 0)
                channel_stats(0, 0)
                channel_spread(0, 0)
                variance(0, 0)
                scale_and_bias(0, 0)
                for c in range(NCH):
                    low_part(0, 0, c)
                make_weights()
                for c in range(NCH):
                    low_part(0, 1, c)
                for m in range(2, 4):
                    for c in range(NCH):
                        stats_piece(0, m, c)
                pieces_made(0, 1)
                channel_stats(0, 1)
                channel_spread(0, 1)
                variance(0, 1)
                scale_and_bias(0, 1)
                for c in range(NCH):
                    stats_piece(0, 4, c)

            def body(it):
                for u in range(U):
                    for c in range(NCH):
                        pair = u % 2 and here(it, u + 3)
                        q = (u + 3) // 2
                        if pair and c == 0:
                            pieces_made(it, q)
                        y_lo(it, u, c)
                        if pair and c == 0:
                            channel_stats(it, q)
                        low_part(it, u + NORM_AHEAD, c)
                        if c:
                            add_residual(it, u, c - 1)
                        elif not isinstance(it, int) or it + u > 0:
                            add_residual(it, u - 1, NCH - 1)
                        stats_piece(it, u + STATS_AHEAD, c)
                        if pair and c == 1:
                            channel_spread(it, q)
                        if pair and c == 3:
                            variance(it, q)
                        if pair and c == 4:
                            scale_and_bias(it, q)

            run(dve, prologue, body)
            add_residual(n_iter - 1, U - 1, NCH - 1)

        @block.tensor
        def _(pe):
            passes = [[] for _ in range(4)]
            for p, (off, _) in enumerate(CEN_PASS):
                passes[0].append((0, off, cen_w16[:, p, :]))
            for i, (g, q, _, _, _) in enumerate(PLACES):
                for p, (off, _) in enumerate(DIR_PASS):
                    passes[q].append((1 + g, off * STEPS[g], dir_w16[:, i, p, :]))

            def depthwise(it, m, c):
                if not here(it, m):
                    return
                e = m % ER
                t = NCH * m + c
                if c == 0:
                    pe.wait_ge(stacked_loaded[m % U], 16 * N_STACK * (it + m // U + 1))
                    pe.wait_ge(centre_stacked, N_CEN * (U * it + m + 1))
                wait(pe, y_lo_made, NCH * U * it + t + 1 - YR)
                for r in range(max(len(x) for x in passes)):
                    for q in range(4):
                        if r < len(passes[q]):
                            tile, off, w = passes[q][r]
                            mm = nc.tensor.matmul(
                                y_ps[32 * q:32 * (q + 1), t % YR, 0:ROWS[c] * HW], w,
                                rows(stacked[:, e, tile, :], BASE + off + ROW0[c] * PITCH, ROWS[c]),
                                start=(r == 0), stop=(r == len(passes[q]) - 1))
                mm.then_inc(y_made, 1)

            def mix(it, u, c):
                t = NCH * u + c
                n = ROWS[c] * HW
                wait(pe, added, NCH * U * it + t + 1 - OR)
                pe.wait_ge(y_lo_made, NCH * U * it + t + 1)
                for k, (w, y) in enumerate(((0, 0), (1, 0), (0, 1))):
                    mm = nc.tensor.matmul(out_ps[:, t % OR, 0:n], mix_w16[:, w, :], y_sb[:, t % YR, y, 0:n],
                                          start=(k == 0), stop=(k == 2))
                mm.then_inc(mixed, 1)

            def means(it, q):
                pe.wait_ge(chan_stats_made, U * it + 2 * q + 2)
                nc.tensor.matmul(stat_ps[:, 0:2], group_mean[:, :], chan_stats[:, :, 0],
                                 start=True, stop=True).then_inc(group_mean_made, 1)

            def variances(it, q):
                pe.wait_ge(spread_made, 3 * (U // 2) * it + 3 * q + 3)
                nc.tensor.matmul(stat_ps[:, 2:4], group_mean[:, :], spread[:, :],
                                 start=True, stop=True).then_inc(group_var_made, 1)

            def prologue():
                pe.wait_ge(masks_made, 1)
                means(0, 0)
                variances(0, 0)
                pe.wait_ge(weights_made, 1)
                depthwise(0, 0, 0)
                means(0, 1)
                variances(0, 1)

            def body(it):
                for u in range(U):
                    pair = u % 2 and here(it, u + 3)
                    q = (u + 3) // 2
                    for c in range(NCH):
                        if c < NCH - 1:
                            depthwise(it, u, c + 1)
                        else:
                            depthwise(it, u + 1, 0)
                        mix(it, u, c)
                        if pair and c == 0:
                            means(it, q)
                        if pair and c == 2:
                            variances(it, q)

            run(pe, prologue, body)


_INS = ["x", "L0_conv_cen_tensor", "L0_conv_dir_tensor", "L0_conv_cen2cen", "L0_conv_par2cen",
        "L0_conv_dia2cen", "L0_conv_cen2dir", "L0_conv_dir2dir"]


def kernel(**inputs):
    import numpy as np
    import concourse.bacc as bacc
    from concourse.bass_utils import run_bass_kernel_spmd

    nc = bacc.Bacc("TRN2", target_bir_lowering=False, num_devices=1)
    arrays, args = {}, []
    for i, name in enumerate(_INS):
        a = np.asarray(inputs[name])
        if i >= 3:
            a = a.T
        a = np.ascontiguousarray(a)
        arrays[f"in_{name}"] = a
        args.append(nc.dram_tensor(f"in_{name}", a.shape, mybir.dt.from_np(a.dtype), kind="ExternalInput").ap())
    x = inputs["x"]
    args.append(nc.dram_tensor("out_0", tuple(x.shape), F32, kind="ExternalOutput").ap())
    build(nc, *args)
    r = run_bass_kernel_spmd(nc, [arrays], core_ids=[0])
    return r.results[0]["out_0"]
```

```python
from contextlib import ExitStack

import concourse.bass as bass
from concourse import mybir

F32 = mybir.dt.float32
F16 = mybir.dt.float16
ALU = mybir.AluOpType
ACT = mybir.ActivationFunctionType
AX = mybir.AxisListType

P = 128
EPS = 1e-5

CEN, DIR = 32, 24
GROUP = 4
HW = 48
PIX = HW * HW

PITCH = HW + 2
BASE = 2 * (PITCH + 1) + 2
SPAN = (HW - 1) * PITCH + HW
LEN = BASE + SPAN + 3 * (PITCH + 1) + 3
LEN += LEN % 2
STEPS = [1, PITCH, PITCH + 1, PITCH - 1]

ROWS = [10, 10, 10, 10, 8]
NCH = len(ROWS)
ROW0 = [sum(ROWS[:c]) for c in range(NCH)]
CHUNK = max(ROWS) * HW

XR = 8
U = 8
NR, ER = 2, 2
YR, OR = 4, 2
ADD_LAG = 3
NORM_AHEAD, STATS_AHEAD, LOAD_AHEAD = 2, 5, 6

DIR_VAR = [("h", 0), ("h", 1), ("h", 2), ("l", 0), ("l", 1)]
DIR_BLOCK = {"h": (0, 3), "l": (3 * DIR, 2)}
DIR_PASS = [
    (-2, [("h", 0), ("h", 1), ("h", 2), ("h", 0), ("h", 1)]),
    (1, [("h", 3), ("h", 4), None, ("h", 3), ("h", 4)]),
    (0, [("l", 2), ("l", 3), ("l", 4), ("h", 2), None]),
    (-2, [("l", 0), ("l", 1), None, None, None]),
]
CEN_VAR = [("h", -1), ("h", 1), ("h", 0), ("l", 0)]
CEN_PASS = []
for _dx in (-1, 0, 1):
    _up, _on, _down = _dx + 1, _dx + 4, _dx + 7
    CEN_PASS += [
        (_dx, [("h", _up), ("h", _down), ("h", _on), ("h", _on)]),
        (_dx + PITCH, [("l", _on), None, ("l", _down), ("h", _down)]),
        (_dx - PITCH, [None, None, ("l", _up), ("h", _up)]),
    ]
Y_SCALE = 16.0

PLACES = []
for _g in range(4):
    _c = 0
    while _c < DIR:
        _at = CEN + DIR * _g + _c
        _n = min(DIR - _c, 32 - _at % 32)
        PLACES.append((_g, _at // 32, _at % 32, _c, _n))
        _c += _n


def build(nc, x_in, cen_k, dir_k, cen2cen_t, par2cen_t, dia2cen_t, cen2dir_t, dir2dir_t, out):
    B = x_in.shape[0]
    n_iter = B // U
    x_d = x_in.rearrange("b c h w -> b c (h w)")
    out_d = out.rearrange("b c h w -> b c (h w)")

    ctx = ExitStack()
    with ctx:
        def sb(name, shape, dt):
            return ctx.enter_context(nc.sbuf_tensor(name, shape, dt))

        def ps(name, shape, dt):
            return ctx.enter_context(nc.psum_tensor(name, shape, dt))

        def sem(name):
            return ctx.enter_context(nc.semaphore(name))

        images = sb("images", [P, XR, PIX], F32)
        split = sb("split", [P, NR, 2, LEN], F16)
        stacked = sb("stacked", [P, ER, 5, LEN], F16)
        xn_piece = sb("xn_piece", [P, 2, CHUNK], F32)
        y_sb = sb("y_sb", [P, YR, 2, CHUNK], F16)

        piece_stats = sb("piece_stats", [P, 4, NCH, 6], F32)
        chan_stats = sb("chan_stats", [P, 2, 2], F32)
        mean_gap = sb("mean_gap", [P, 2], F32)
        spread = sb("spread", [P, 2], F32)
        var_eps = sb("var_eps", [P, 2], F32)
        unused = sb("unused", [P, 1], F32)
        std = sb("std", [P, 2], F32)
        inv0 = sb("inv0", [P, 2], F32)
        newton = sb("newton", [P, 3, 2], F32)
        norm_scale = sb("norm_scale", [P, 4, 2], F32)
        norm_bias = sb("norm_bias", [P, 4, 2], F32)

        group_mean = sb("group_mean", [P, P], F32)
        mix_w = sb("mix_w", [P, P], F32)
        mix_hi32 = sb("mix_hi32", [P, P], F32)
        mix_w16 = sb("mix_w16", [P, 2, 4, P], F16)
        dir_sel = sb("dir_sel", [P, len(DIR_VAR), DIR], F32)
        cen_sel = sb("cen_sel", [P, len(CEN_VAR), CEN], F32)
        dir_taps = sb("dir_taps", [P, 5], F32)
        cen_taps = sb("cen_taps", [P, 9], F32)
        nat_taps = sb("nat_taps", [P, 9], F32)
        row_max = sb("row_max", [P, 4], F32)
        row_inv = sb("row_inv", [P, 4], F32)
        y_scale = sb("y_scale", [P, 4], F32)
        dir_tap16 = sb("dir_tap16", [P, 2, 5], F16)
        cen_tap16 = sb("cen_tap16", [P, 2, 9], F16)
        dir_part = sb("dir_part", [P, 2, 5], F32)
        cen_part = sb("cen_part", [P, 2, 9], F32)
        dir_lane = sb("dir_lane", [P, len(DIR_VAR)], F32)
        cen_lane = sb("cen_lane", [P, len(CEN_VAR)], F32)
        dir_diag = sb("dir_diag", [P, DIR], F32)
        cen_diag = sb("cen_diag", [P, CEN], F32)
        dir_coef = sb("dir_coef", [P, len(DIR_PASS)], F32)
        cen_coef = sb("cen_coef", [P, len(CEN_PASS)], F32)
        dir_w = sb("dir_w", [P, len(DIR_PASS), DIR], F32)
        cen_w16 = sb("cen_w16", [P, len(CEN_PASS), CEN], F16)
        dir_w16 = sb("dir_w16", [P, len(PLACES), len(DIR_PASS), 32], F16)

        y_ps = ps("y_ps", [P, YR, 512], F32)
        out_ps = ps("out_ps", [P, OR, 512], F32)
        stat_ps = ps("stat_ps", [P, 512], F32)

        taps_loaded = sem("taps_loaded")
        mix_loaded = sem("mix_loaded")
        masks_made = sem("masks_made")
        mix_parted = sem("mix_parted")
        mix_copied = sem("mix_copied")
        y_scale_made = sem("y_scale_made")
        y_scale_copied = sem("y_scale_copied")
        selectors_made = sem("selectors_made")
        pool_step = sem("pool_step")
        tables_zeroed = sem("tables_zeroed")
        padding_zeroed = sem("padding_zeroed")
        lanes_zeroed = sem("lanes_zeroed")
        stats_made = sem("stats_made")
        newton_step = sem("newton_step")
        weights_made = sem("weights_made")
        dve_step = sem("dve_step")
        loaded = [sem(f"loaded{s}") for s in range(XR)]
        stored = [sem(f"stored{s}") for s in range(XR)]
        chan_stats_made = sem("chan_stats_made")
        group_mean_made = sem("group_mean_made")
        spread_made = sem("spread_made")
        group_var_made = sem("group_var_made")
        var_eps_made = sem("var_eps_made")
        std_made = sem("std_made")
        norm_ready = sem("norm_ready")
        xn_made = sem("xn_made")
        hi_made = sem("hi_made")
        lo_made = sem("lo_made")
        stacked_loaded = [sem(f"stacked_loaded{s}") for s in range(U)]
        y_made = sem("y_made")
        y_hi_made = sem("y_hi_made")
        y_lo_made = sem("y_lo_made")
        centre_stacked = sem("centre_stacked")
        centre_zeroed = sem("centre_zeroed")
        centre_down = sem("centre_down")
        centre_up = sem("centre_up")
        pool_tick = sem("pool_tick")
        mixed = sem("mixed")
        added = sem("added")

        N_STACK = 4 * len(DIR_BLOCK)
        N_TURNS = 3 * 4
        N_UP = 3

        N_CEN = NCH * 2

        def rows(ap, start, n):
            return ap[:, start:start + n * PITCH].rearrange("p (r w) -> p r w", w=PITCH)[:, :, 0:HW]

        def pixels(ap, c):
            return ap[:, ROW0[c] * HW:(ROW0[c] + ROWS[c]) * HW]

        def here(it, m):
            return not isinstance(it, int) or U * it + m < B

        def begins(it, u):
            return isinstance(it, int) and U * it + u == 0

        def wait(eng, s, count):
            if not isinstance(count, int) or count > 0:
                eng.wait_ge(s, count)

        def run(eng, prologue, body):
            prologue()
            body(0)
            with eng.Fori(1, n_iter - 1) as it:
                body(it)
            body(n_iter - 1)

        block = ctx.enter_context(nc.Block())

        @block.sync
        def _(sp):
            def load(it, m):
                if here(it, m):
                    s = m % XR
                    if isinstance(it, int):
                        wait(sp, stored[s], 16 * (it + m // U))
                    else:
                        sp.wait_ge(stored[s], 16 * it + 16 * (m // U))
                    sp.dma_start(images[:, s, :], x_d[it * U + m, :, :]).then_inc(loaded[s], 16)

            def stack(it, m):
                if not here(it, m):
                    return
                n, e = m % NR, m % ER
                wait(sp, lo_made, NCH * U * it + NCH * (m + 1))
                if begins(it, m - NORM_AHEAD):
                    sp.wait_ge(y_lo_made, NCH)
                done = stacked_loaded[m % U]
                for k, (first, nv) in enumerate(DIR_BLOCK.values()):
                    for g, step in enumerate(STEPS):
                        a, b = BASE - 2 * step, BASE + SPAN + step
                        src = split[CEN + DIR * g:CEN + DIR * (g + 1), n, k, a:b]
                        src = bass.AP(tensor=src.tensor, offset=src.offset,
                                      ap=[src.ap[0], [step, nv], src.ap[1]])
                        sp.dma_start(stacked[first:first + nv * DIR, e, 1 + g, a:b], src).then_inc(done, 16)

            def store(it, m):
                s = m % XR
                wait(sp, added, NCH * U * it + NCH * (m + 1))
                sp.dma_start(out_d[it * U + m, :, :], images[:, s, :]).then_inc(stored[s], 16)

            def repeated(src, n):
                return bass.AP(tensor=src.tensor, offset=src.offset, ap=[[0, n]] + list(src.ap))

            def prologue():
                load(0, 0)
                sp.wait_ge(tables_zeroed, 3)
                for first, nv in DIR_BLOCK.values():
                    src = bass.AP(tensor=dir_k.tensor, offset=dir_k.offset, ap=[dir_k.ap[0], [0, nv], dir_k.ap[1]])
                    sp.dma_start(dir_taps[first:first + nv * DIR, :], src).then_inc(taps_loaded, 16)
                cen_k2 = cen_k.rearrange("c a b -> c (a b)")
                sp.dma_start(cen_taps[:, :], repeated(cen_k2, len(CEN_VAR))).then_inc(taps_loaded, 16)
                sp.dma_start(nat_taps[0:CEN, :], cen_k2).then_inc(taps_loaded, 16)
                sp.dma_start(nat_taps[CEN:P, 0:5], repeated(dir_k, 4)).then_inc(taps_loaded, 16)
                load(0, 1)
                sp.dma_start(mix_w[0:CEN, 0:CEN], cen2cen_t).then_inc(mix_loaded, 16)
                src = bass.AP(tensor=cen2dir_t.tensor, offset=cen2dir_t.offset,
                              ap=[cen2dir_t.ap[0], [0, 4], cen2dir_t.ap[1]])
                sp.dma_start(mix_w[0:CEN, CEN:P].rearrange("c (g d) -> c g d", g=4), src).then_inc(mix_loaded, 16)
                sp.dma_start(mix_w[CEN:CEN + 2 * DIR, 0:CEN], repeated(par2cen_t, 2)).then_inc(mix_loaded, 16)
                sp.dma_start(mix_w[CEN + 2 * DIR:P, 0:CEN], repeated(dia2cen_t, 2)).then_inc(mix_loaded, 16)
                for g in range(4):
                    c0 = CEN + DIR * g
                    sp.dma_start(mix_w[c0:c0 + DIR, c0:c0 + DIR], dir2dir_t).then_inc(mix_loaded, 16)
                load(0, 2)
                load(0, 3)
                sp.wait_ge(lanes_zeroed, 1)
                stack(0, 0)

            def body(it):
                for u in range(U):
                    stack(it, u + 1)
                    if isinstance(it, int) and it + u == 0:
                        load(0, 4)
                        load(0, 5)
                    load(it, u + LOAD_AHEAD)
                    if not isinstance(it, int) or it * U + u > 0:
                        store(it, u - 1) if u else store(it - 1, U - 1)

            run(sp, prologue, body)
            store(n_iter - 1, U - 1)
            for s in range(XR):
                sp.wait_ge(stored[s], 16 * (B // XR))

        @block.gpsimd
        def _(pool):
            count = [0]

            def link(ins):
                count[0] += 1
                ins.then_inc(pool_step, 1)
                pool.wait_ge(pool_step, count[0])

            for i, table in enumerate((mix_w, nat_taps, dir_taps)):
                nc.gpsimd.memset(table[:], 0.0).then_inc(tables_zeroed, 1)
                pool.wait_ge(tables_zeroed, i + 1)
            link(nc.gpsimd.memset(dir_sel[:], 0.0))
            link(nc.gpsimd.memset(cen_sel[:], 0.0))
            link(nc.gpsimd.memset(group_mean[:], 1.0 / GROUP))
            dir_start = [(first + k, nv) for first, nv in DIR_BLOCK.values() for k in range(nv)]
            cen_start = [(CEN * v, 1) for v in range(len(CEN_VAR))]
            for sel, starts, cols in ((dir_sel, dir_start, DIR), (cen_sel, cen_start, CEN)):
                for v, (start, nv) in enumerate(starts):
                    link(nc.gpsimd.affine_select(
                        out=sel[:, v, :], in_=sel[:, v, :], compare_op=ALU.not_equal, fill=1.0,
                        base=-start, pattern=[[-nv, cols]], channel_multiplier=1))
            pool.sem_inc(selectors_made, 1)
            gv = group_mean[:, :].rearrange("p (a b) -> p a b", b=GROUP)
            link(nc.gpsimd.affine_select(
                out=gv, in_=gv, compare_op=ALU.is_ge, fill=0.0,
                base=0, pattern=[[-GROUP, P // GROUP], [0, GROUP]], channel_multiplier=1))
            nc.gpsimd.affine_select(
                out=gv, in_=gv, compare_op=ALU.is_ge, fill=0.0,
                base=GROUP - 1, pattern=[[GROUP, P // GROUP], [0, GROUP]],
                channel_multiplier=-1).then_inc(masks_made, 1)
            pool.wait_ge(masks_made, 1)
            nc.gpsimd.memset(stacked[96:P, :, 1:5, :].bitcast(mybir.dt.uint32), 0).then_inc(lanes_zeroed, 1)
            pool.wait_ge(lanes_zeroed, 1)
            nc.gpsimd.memset(stacked[:, :, 0, :].bitcast(mybir.dt.uint32), 0).then_inc(centre_zeroed, 1)
            pool.wait_ge(centre_zeroed, 1)

            def stack_centre(it, m):
                if not here(it, m):
                    return
                n, e = m % NR, m % ER
                first = begins(it, m)
                if begins(it, m - NORM_AHEAD):
                    pool.wait_ge(y_lo_made, NCH)
                if not first:
                    wait(pool, lo_made, NCH * U * it + NCH * (m + 1))
                    pool.sem_inc(pool_tick, 1)
                for c in range(NCH):
                    if first:
                        pool.wait_ge(lo_made, c + 1)
                    a = BASE + ROW0[c] * PITCH
                    b = a + ROWS[c] * PITCH
                    for v, (part, shift) in enumerate(CEN_VAR):
                        if shift == 0:
                            nc.gpsimd.tensor_copy(
                                stacked[CEN * v:CEN * (v + 1), e, 0, a:b].bitcast(mybir.dt.uint32),
                                split[0:CEN, n, "hl".index(part), a:b].bitcast(mybir.dt.uint32)
                            ).then_inc(centre_stacked, 1)

            def body(it):
                for u in range(U):
                    stack_centre(it, u + 1)

            def prologue():
                turns = [(v, slice(32 * to, 32 * to + 32), slice(32 * at, 32 * at + 32)) for v in range(1, 4)
                         for to, at in ((0, v), (v, 0), *((q, q) for q in range(1, 4) if q != v))]
                pool.wait_ge(y_scale_made, 1)
                for v, a, b in turns:
                    nc.gpsimd.tensor_copy(y_scale[a, v:v + 1], y_scale[b, 0:1]).then_inc(y_scale_copied, 1)
                stack_centre(0, 0)
                pool.wait_ge(mix_parted, 1)
                for v, a, b in turns:
                    nc.gpsimd.tensor_copy(mix_w16[a, :, v, :].bitcast(mybir.dt.uint32),
                                          mix_w16[b, :, 0, :].bitcast(mybir.dt.uint32)).then_inc(mix_copied, 1)

            run(pool, prologue, body)

        @block.scalar
        def _(act):
            def normalise(it, m, c):
                if not here(it, m):
                    return
                s, n, pair, k = m % XR, m % NR, (m // 2) % 4, m % 2
                t = NCH * m + c
                if c == 0:
                    wait(act, norm_ready, U // 2 * it + m // 2 + 1)
                    if not isinstance(it, int) or it * U + m >= NR:
                        mm = m - NR
                        act.wait_ge(stacked_loaded[mm % U], 16 * N_STACK * (it + mm // U + 1))
                        act.wait_ge(centre_stacked, N_CEN * (U * it + mm + 1))
                        act.wait_ge(centre_down, U * it + mm + 1)
                        act.wait_ge(centre_up, N_UP * (U * it + mm + 1))
                bias, scale = norm_bias[:, pair, k:k + 1], norm_scale[:, pair, k:k + 1]
                wait(act, lo_made, NCH * U * it + t + 1 - 2)
                px = pixels(images[:, s, :], c)
                nc.scalar.activation(xn_piece[:, t % 2, 0:ROWS[c] * HW], px, ACT.Identity,
                                     bias=bias, scale=scale).then_inc(xn_made, 1)
                nc.scalar.activation(rows(split[:, n, 0, :], BASE + ROW0[c] * PITCH, ROWS[c]),
                                     px.rearrange("p (r w) -> p r w", w=HW), ACT.Identity,
                                     bias=bias, scale=scale).then_inc(hi_made, 1)

            def y_hi(it, u, c):
                t = NCH * u + c
                n = ROWS[c] * HW
                wait(act, mixed, NCH * U * it + t + 1 - YR)
                act.wait_ge(y_made, NCH * U * it + t + 1)
                nc.scalar.activation(y_sb[:, t % YR, 0, 0:n], y_ps[:, t % YR, 0:n], ACT.Identity,
                                     scale=y_scale[:, t % 4:t % 4 + 1]).then_inc(y_hi_made, 1)

            def deviation(it, q):
                act.wait_ge(var_eps_made, U // 2 * it + q + 1)
                nc.scalar.activation(std[:, :], var_eps[:, :], ACT.Sqrt).then_inc(std_made, 1)

            def centre_row_up(it, m, k):
                if not here(it, m):
                    return
                n, e = m % NR, m % ER
                act.wait_ge(hi_made, NCH * U * it + NCH * (m + 1))
                size = HW // N_UP * PITCH
                first, at = CEN * CEN_VAR.index(("h", 1)), BASE + k * size
                nc.scalar.activation(stacked[first:first + CEN, e, 0, at - PITCH:at - PITCH + size],
                                     split[0:CEN, n, 0, at:at + size], ACT.Identity).then_inc(centre_up, 1)

            def prologue():
                act.wait_ge(padding_zeroed, 1)
                nc.scalar.activation(unused[:, :], split[:, 0, 0, 0:1], ACT.Sqrt)
                deviation(0, 0)
                for m in range(2):
                    for c in range(NCH):
                        normalise(0, m, c)
                act.wait_ge(centre_zeroed, 1)
                for k in range(N_UP):
                    centre_row_up(0, 0, k)
                deviation(0, 1)
                for c in range(NCH):
                    normalise(0, NORM_AHEAD, c)
                act.wait_ge(y_scale_copied, N_TURNS)

            def body(it):
                for u in range(U):
                    for c in range(NCH):
                        y_hi(it, u, c)
                        if not begins(it, u):
                            normalise(it, u + NORM_AHEAD, c)
                        if c < N_UP:
                            centre_row_up(it, u + 1, c)
                        if c == NCH - 1 and u % 2 and here(it, u + 3):
                            deviation(it, (u + 3) // 2)

            run(act, prologue, body)

        @block.vector
        def _(dve):
            count = [0]

            def link(ins):
                count[0] += 1
                ins.then_inc(dve_step, 1)
                dve.wait_ge(dve_step, count[0])

            def stats_piece(it, m, c):
                if not here(it, m):
                    return
                s = m % XR
                if c == 0:
                    dve.wait_ge(loaded[s], 16 * (it + m // U + 1))
                nc.vector.bn_stats(piece_stats[:, m % 4, c, :], pixels(images[:, s, :], c)).then_inc(stats_made, 1)

            def pieces_made(it, q):
                dve.wait_ge(stats_made, NCH * U * it + 2 * NCH * (q + 1))

            def channel_stats(it, q):
                for k in range(2):
                    nc.vector.bn_aggr(chan_stats[:, k, :], piece_stats[:, (2 * q + k) % 4, :, :]).then_inc(chan_stats_made, 1)

            def channel_spread(it, q):
                n = U // 2 * it + q
                means, vars_ = chan_stats[:, :, 0], chan_stats[:, :, 1]
                dve.wait_ge(group_mean_made, n + 1)
                nc.vector.tensor_tensor(mean_gap[:, :], means, stat_ps[:, 0:2], ALU.subtract).then_inc(spread_made, 1)
                dve.wait_ge(spread_made, 3 * n + 1)
                nc.vector.tensor_tensor(mean_gap[:, :], mean_gap[:, :], mean_gap[:, :], ALU.mult).then_inc(spread_made, 1)
                dve.wait_ge(spread_made, 3 * n + 2)
                nc.vector.tensor_tensor(spread[:, :], mean_gap[:, :], vars_, ALU.add).then_inc(spread_made, 1)

            def variance(it, q):
                n = U // 2 * it + q
                dve.wait_ge(group_var_made, n + 1)
                nc.vector.tensor_scalar(var_eps[:, :], stat_ps[:, 2:4], EPS, None, ALU.add).then_inc(var_eps_made, 1)

            def scale_and_bias(it, q):
                n = U // 2 * it + q
                dve.wait_ge(std_made, n + 1)
                nc.vector.reciprocal(inv0[:, :], std[:, :]).then_inc(newton_step, 1)
                dve.wait_ge(newton_step, 5 * n + 1)
                nc.vector.tensor_tensor(newton[:, 0, :], inv0[:, :], inv0[:, :], ALU.mult).then_inc(newton_step, 1)
                dve.wait_ge(newton_step, 5 * n + 2)
                nc.vector.tensor_tensor(newton[:, 1, :], newton[:, 0, :], var_eps[:, :], ALU.mult).then_inc(newton_step, 1)
                dve.wait_ge(newton_step, 5 * n + 3)
                nc.vector.tensor_scalar(newton[:, 2, :], newton[:, 1, :], -0.5, 1.5, ALU.mult, ALU.add).then_inc(newton_step, 1)
                dve.wait_ge(newton_step, 5 * n + 4)
                nc.vector.tensor_tensor(norm_scale[:, q % 4, :], newton[:, 2, :], inv0[:, :], ALU.mult).then_inc(newton_step, 1)
                dve.wait_ge(newton_step, 5 * n + 5)
                nc.vector.scalar_tensor_tensor(norm_bias[:, q % 4, :], stat_ps[:, 0:2], -1.0,
                                               norm_scale[:, q % 4, :], ALU.mult, ALU.mult).then_inc(norm_ready, 1)

            def low_part(it, m, c):
                if not here(it, m):
                    return
                n = m % NR
                t = NCH * m + c
                dve.wait_ge(hi_made, NCH * U * it + t + 1)
                at = BASE + ROW0[c] * PITCH
                nc.vector.tensor_tensor(
                    rows(split[:, n, 1, :], at, ROWS[c]),
                    xn_piece[:, t % 2, 0:ROWS[c] * HW].rearrange("p (r w) -> p r w", w=HW),
                    rows(split[:, n, 0, :], at, ROWS[c]), ALU.subtract).then_inc(lo_made, 1)

            def y_lo(it, u, c):
                t = NCH * u + c
                n = ROWS[c] * HW
                dve.wait_ge(y_hi_made, NCH * U * it + t + 1)
                nc.vector.scalar_tensor_tensor(y_sb[:, t % YR, 1, 0:n], y_ps[:, t % YR, 0:n],
                                               y_scale[:, t % 4:t % 4 + 1],
                                               y_sb[:, t % YR, 0, 0:n], ALU.mult, ALU.subtract).then_inc(y_lo_made, 1)

            def add_residual(it, u, c):
                t = NCH * u + c
                dve.wait_ge(mixed, NCH * U * it + t + 1)
                px = pixels(images[:, u % XR, :], c)
                nc.vector.scalar_tensor_tensor(px, out_ps[:, t % OR, 0:ROWS[c] * HW], 1.0 / Y_SCALE, px,
                                               ALU.mult, ALU.add).then_inc(added, 1)

            def centre_row_down(it, m):
                if not here(it, m):
                    return
                n, e = m % NR, m % ER
                dve.wait_ge(hi_made, NCH * U * it + NCH * (m + 1))
                first, at = CEN * CEN_VAR.index(("h", -1)), BASE + PITCH
                nc.vector.tensor_copy(stacked[first:first + CEN, e, 0, at:at + HW * PITCH],
                                      split[0:CEN, n, 0, BASE:BASE + HW * PITCH]).then_inc(centre_down, 1)

            def part_taps(pairs):
                for taps, _, _, inv in pairs:
                    last = nc.vector.tensor_scalar(taps[:], taps[:], inv, None, ALU.mult)
                link(last)
                for taps, _, tap16, _ in pairs:
                    last = nc.vector.tensor_copy(tap16[:, 0, :], taps[:])
                link(last)
                for taps, part, tap16, _ in pairs:
                    last = nc.vector.tensor_copy(part[:, 0, :], tap16[:, 0, :])
                link(last)
                for taps, part, tap16, _ in pairs:
                    last = nc.vector.tensor_tensor(tap16[:, 1, :], taps[:], part[:, 0, :], ALU.subtract)
                link(last)
                for taps, part, tap16, _ in pairs:
                    last = nc.vector.tensor_copy(part[:, 1, :], tap16[:, 1, :])
                link(last)

            def uses_of(passes, v):
                todo = [(p, *uses[v]) for p, (_, uses) in enumerate(passes) if uses[v] is not None]
                while todo:
                    same = [x for x in todo if x[1] == todo[0][1]]
                    run_ = same[:2]
                    for x in same[2:]:
                        if (x[0] - run_[-1][0], x[2] - run_[-1][2]) == (run_[1][0] - run_[0][0], run_[1][2] - run_[0][2]):
                            run_.append(x)
                    todo = [x for x in todo if x not in run_]
                    yield [x[0] for x in run_], run_[0][1], [x[2] for x in run_]

            def evenly(ap, at):
                step = at[1] - at[0] if len(at) > 1 else 1
                first = ap[:, at[0]:at[0] + 1]
                return bass.AP(tensor=first.tensor, offset=first.offset, ap=[first.ap[0], [step, len(at)]])

            dir_steps = [(v, *x) for v in range(len(DIR_VAR)) for x in uses_of(DIR_PASS, v)]
            cen_steps = [(v, *x) for v in range(len(CEN_VAR)) for x in uses_of(CEN_PASS, v)]
            n_steps = max(len(dir_steps), len(cen_steps))

            def coefficients(i):
                for steps, coef, part, lane in ((dir_steps, dir_coef, dir_part, dir_lane),
                                                (cen_steps, cen_coef, cen_part, cen_lane)):
                    if i < len(steps):
                        v, at, kind, taps = steps[i]
                        out_ = evenly(coef[:, :], at)
                        last = nc.vector.scalar_tensor_tensor(
                            out_, evenly(part[:, "hl".index(kind), :], taps), lane[:, v:v + 1], out_,
                            ALU.mult, ALU.add)
                link(last)

            def lane_tables():
                nc.vector.memset(dir_coef[:], 0.0)
                nc.vector.memset(cen_coef[:], 0.0)
                nc.vector.memset(dir_w16[:], 0.0)
                dve.wait_ge(selectors_made, 1)
                nc.vector.tensor_reduce(dir_lane[:, :], dir_sel[:], AX.X, ALU.add)
                nc.vector.tensor_reduce(cen_lane[:, :], cen_sel[:], AX.X, ALU.add)
                nc.vector.tensor_reduce(dir_diag[:, :], dir_sel[:].rearrange("p v c -> p c v"), AX.X, ALU.add)
                nc.vector.tensor_reduce(cen_diag[:, :], cen_sel[:].rearrange("p v c -> p c v"), AX.X, ALU.add)

            def row_maxima():
                dve.wait_ge(taps_loaded, 16 * 5)
                dve.wait_ge(mix_loaded, 16 * 8)
                for col, table in enumerate((dir_taps, cen_taps, nat_taps, mix_w)):
                    last = nc.vector.tensor_reduce(row_max[:, col:col + 1], table[:], AX.X, ALU.max,
                                                   apply_absolute_value=True)
                link(last)
                link(nc.vector.tensor_scalar(row_max[:, :], row_max[:, :], 1e-30, None, ALU.max))
                nc.vector.scalar_tensor_tensor(y_scale[:, 0:1], row_max[:, 2:3], Y_SCALE, row_max[:, 3:4],
                                               ALU.mult, ALU.mult).then_inc(y_scale_made, 1)
                link(nc.vector.reciprocal(row_inv[:, :], row_max[:, :]))

            def part_mix():
                link(nc.vector.tensor_scalar(mix_w[:], mix_w[:], row_inv[:, 3:4], None, ALU.mult))
                link(nc.vector.tensor_copy(mix_w16[:, 0, 0, :], mix_w[:]))
                link(nc.vector.tensor_copy(mix_hi32[:], mix_w16[:, 0, 0, :]))
                nc.vector.tensor_tensor(mix_w16[:, 1, 0, :], mix_w[:], mix_hi32[:], ALU.subtract).then_inc(mix_parted, 1)

            def weight_tables():
                for w, diag, coef, passes, cols in ((dir_w, dir_diag, dir_coef, DIR_PASS, DIR),
                                                    (cen_w16, cen_diag, cen_coef, CEN_PASS, CEN)):
                    n = len(passes)
                    d, k = diag[:, :], coef[:, :]
                    last = nc.vector.tensor_tensor(
                        w[:], bass.AP(tensor=d.tensor, offset=d.offset, ap=[d.ap[0], [0, n], [1, cols]]),
                        bass.AP(tensor=k.tensor, offset=k.offset, ap=[k.ap[0], [1, n], [0, cols]]), ALU.mult)
                link(last)
                for i, (g, q, col, ch, n) in enumerate(PLACES):
                    last = nc.vector.tensor_copy(dir_w16[:, i, :, col:col + n], dir_w[:, :, ch:ch + n])
                last.then_inc(weights_made, 1)

            def prologue():
                nc.vector.memset(split[:, :, :, 0:BASE], 0.0)
                nc.vector.memset(split[:, :, :, BASE + SPAN:LEN], 0.0)
                for n in range(NR):
                    gaps = split[:, n, :, BASE + HW:BASE + HW + PITCH * (HW - 1)]
                    last = nc.vector.memset(gaps.rearrange("p k (r w) -> p k r w", w=PITCH)[:, :, :, 0:2], 0.0)
                last.then_inc(padding_zeroed, 1)
                lane_tables()
                for m in range(2):
                    for c in range(NCH):
                        stats_piece(0, m, c)
                pieces_made(0, 0)
                channel_stats(0, 0)
                row_maxima()
                channel_spread(0, 0)
                variance(0, 0)
                part_taps([(dir_taps, dir_part, dir_tap16, row_inv[:, 0:1]),
                           (cen_taps, cen_part, cen_tap16, row_inv[:, 1:2])])
                scale_and_bias(0, 0)
                for m in range(2):
                    for c in range(NCH):
                        low_part(0, m, c)
                        for i in range(n_steps * (NCH * m + c) // (2 * NCH), n_steps * (NCH * m + c + 1) // (2 * NCH)):
                            coefficients(i)
                        stats_piece(0, 2 + m, c)
                pieces_made(0, 1)
                channel_stats(0, 1)
                part_mix()
                channel_spread(0, 1)
                dve.wait_ge(centre_zeroed, 1)
                centre_row_down(0, 0)
                dve.wait_ge(y_scale_copied, N_TURNS)
                variance(0, 1)
                weight_tables()
                scale_and_bias(0, 1)
                for c in range(NCH):
                    low_part(0, NORM_AHEAD, c)

            def add_earlier(it, u, c):
                t = NCH * u + c - ADD_LAG
                if not isinstance(it, int) or NCH * U * it + t >= 0:
                    add_residual(it, t // NCH, t % NCH)

            def body(it):
                for u in range(U):
                    for c in range(NCH):
                        pair = u % 2 and here(it, u + 3)
                        q = (u + 3) // 2
                        even = (NCH * u + c) % 2 == 0
                        if even:
                            add_earlier(it, u, c)
                        y_lo(it, u, c)
                        if pair and c == 0:
                            pieces_made(it, q)
                        if pair and c == 4:
                            variance(it, q)
                        if not begins(it, u):
                            low_part(it, u + NORM_AHEAD, c)
                        if pair and c == 0:
                            channel_stats(it, q)
                        if not even:
                            add_earlier(it, u, c)
                        if pair and c == 2:
                            channel_spread(it, q)
                        if pair and c == 4:
                            scale_and_bias(it, q)
                        if c == 0:
                            centre_row_down(it, u + 1)
                        if isinstance(it, int) and it + u == 0:
                            stats_piece(it, u + STATS_AHEAD - 1, c)
                        stats_piece(it, u + STATS_AHEAD, c)

            run(dve, prologue, body)
            for c in range(NCH - ADD_LAG, NCH):
                add_residual(n_iter - 1, U - 1, c)

        @block.tensor
        def _(pe):
            passes = [[] for _ in range(4)]
            for p, (off, _) in enumerate(CEN_PASS):
                passes[0].append((0, off, cen_w16[:, p, :]))
            for i, (g, q, _, _, _) in enumerate(PLACES):
                for p, (off, _) in enumerate(DIR_PASS):
                    passes[q].append((1 + g, off * STEPS[g], dir_w16[:, i, p, :]))

            def depthwise_pair(it, p):
                todo = [[] for _ in range(4)]
                for t in range(2 * (p - p % 2), 2 * (p - p % 2) + 4):
                    if here(it, t // NCH):
                        for q in range(4):
                            own = passes[0 if q == t % 4 else t % 4 if q == 0 else q]
                            todo[q] += [(t, q, k, len(own), *own[k]) for k in range(len(own))]
                n_rounds = max(len(x) for x in todo)
                order = [(r, *x[r]) for r in range(n_rounds) for x in todo if r < len(x)]
                chunks = [x[1] for x in order]
                half = range(n_rounds // 2 + 1) if p % 2 == 0 else range(n_rounds // 2 + 1, n_rounds)
                for n, (r, t, q, k, n_own, tile, off, w) in enumerate(order):
                    if r not in half:
                        continue
                    m, c = t // NCH, t % NCH
                    if t not in chunks[:n]:
                        if c == 0:
                            pe.wait_ge(stacked_loaded[m % U], 16 * N_STACK * (it + m // U + 1))
                            pe.wait_ge(centre_down, U * it + m + 1)
                            pe.wait_ge(centre_up, N_UP * (U * it + m + 1))
                        pe.wait_ge(centre_stacked, N_CEN * (U * it + m) + N_CEN // NCH * min(c + 2, NCH))
                        wait(pe, y_lo_made, NCH * U * it + t + 1 - YR)
                    mm = nc.tensor.matmul(
                        y_ps[32 * q:32 * (q + 1), t % YR, 0:ROWS[c] * HW], w,
                        rows(stacked[:, m % ER, tile, :], BASE + off + ROW0[c] * PITCH, ROWS[c]),
                        start=(k == 0), stop=(k == n_own - 1))
                    if t not in chunks[n + 1:]:
                        mm.then_inc(y_made, 1)

            def mix(it, u, c):
                t = NCH * u + c
                n = ROWS[c] * HW
                wait(pe, added, NCH * U * it + t + 1 - OR)
                pe.wait_ge(y_lo_made, NCH * U * it + t + 1)
                for k, (w, y) in enumerate(((0, 0), (1, 0), (0, 1))):
                    mm = nc.tensor.matmul(out_ps[:, t % OR, 0:n], mix_w16[:, w, t % 4, :], y_sb[:, t % YR, y, 0:n],
                                          start=(k == 0), stop=(k == 2))
                mm.then_inc(mixed, 1)

            def means(it, q):
                pe.wait_ge(chan_stats_made, U * it + 2 * q + 2)
                nc.tensor.matmul(stat_ps[:, 0:2], group_mean[:, :], chan_stats[:, :, 0],
                                 start=True, stop=True).then_inc(group_mean_made, 1)

            def variances(it, q):
                pe.wait_ge(spread_made, 3 * (U // 2) * it + 3 * q + 3)
                nc.tensor.matmul(stat_ps[:, 2:4], group_mean[:, :], spread[:, :],
                                 start=True, stop=True).then_inc(group_var_made, 1)

            def prologue():
                pe.wait_ge(masks_made, 1)
                means(0, 0)
                variances(0, 0)
                means(0, 1)
                variances(0, 1)
                pe.wait_ge(weights_made, 1)
                depthwise_pair(0, 0)
                pe.wait_ge(mix_copied, N_TURNS)

            def body(it):
                for p in range(NCH * U // 2):
                    depthwise_pair(it, p + 1)
                    for t in (2 * p + 2, 2 * p + 3):
                        u, c = t // NCH, t % NCH
                        if u < U and u % 2 and here(it, u + 3):
                            if c == 1:
                                means(it, (u + 3) // 2)
                            if c == 4:
                                variances(it, (u + 3) // 2)
                    for t in (2 * p, 2 * p + 1):
                        mix(it, t // NCH, t % NCH)

            run(pe, prologue, body)


_INS = ["x", "L0_conv_cen_tensor", "L0_conv_dir_tensor", "L0_conv_cen2cen", "L0_conv_par2cen",
        "L0_conv_dia2cen", "L0_conv_cen2dir", "L0_conv_dir2dir"]


def kernel(**inputs):
    import numpy as np
    import concourse.bacc as bacc
    from concourse.bass_utils import run_bass_kernel_spmd

    nc = bacc.Bacc("TRN2", target_bir_lowering=False, num_devices=1)
    arrays, args = {}, []
    for i, name in enumerate(_INS):
        a = np.asarray(inputs[name])
        if i >= 3:
            a = a.T
        a = np.ascontiguousarray(a)
        arrays[f"in_{name}"] = a
        args.append(nc.dram_tensor(f"in_{name}", a.shape, mybir.dt.from_np(a.dtype), kind="ExternalInput").ap())
    x = inputs["x"]
    args.append(nc.dram_tensor("out_0", tuple(x.shape), F32, kind="ExternalOutput").ap())
    build(nc, *args)
    r = run_bass_kernel_spmd(nc, [arrays], core_ids=[0])
    return r.results[0]["out_0"]
```
